# Optimizing a Trainium2 kernel written in Bass

```python
import numpy as np
import jax
import jax.numpy as jnp

def _softmax(x, axis=-1):
    return jax.nn.softmax(x, axis=axis)

def _gelu(x):
    return jax.nn.gelu(x, approximate=True)

def _silu(x):
    return jax.nn.silu(x)

def _sigmoid(x):
    return jax.nn.sigmoid(x)

def _layernorm(x, axis=-1, eps=1e-05):
    m = jnp.mean(x, axis=axis, keepdims=True)
    v = jnp.var(x, axis=axis, keepdims=True)
    return (x - m) / jnp.sqrt(v + eps)

def _scatter_add(tgt, idx, src, axis=0):
    return tgt.at[idx].add(src)

def _segment_sum(src, seg, n):
    return jax.ops.segment_sum(src, seg, n)
kernel_name = 'mk_gnn_resnorm_d1_gnn_r8_14d9f1'

def setup_inputs(seed: int=0):
    np.random.seed(seed)
    _w = jnp.asarray

    def _rec_inputs():
        import jax
        import jax.numpy as jnp
        _gk = jax.random.key(seed)
        x = -0.0006008 + 1.001 * jax.random.normal(jax.random.fold_in(_gk, 1), (6250, 256), jnp.float32)
        src = jax.random.randint(jax.random.fold_in(_gk, 2), (100000,), 0, 6250, jnp.int32)
        dst = jax.random.randint(jax.random.fold_in(_gk, 3), (100000,), 0, 6250, jnp.int32)
        _o = jnp.argsort(dst, stable=True)
        src = src[_o]
        dst = dst[_o]
        return (x, src, dst)
    x, src, dst = _rec_inputs()

    def _L0_gnn_setup():
        import jax, jax.numpy as jnp
        import numpy as np
        N_NODES = 1250
        N_EDGES = 40000
        D = 256
        key = jax.random.key(seed)
        k1, k2, k3, k4, k5 = jax.random.split(key, 5)
        x = jax.random.normal(k1, (N_NODES, D), dtype=jnp.float32)
        src = jax.random.randint(k2, (N_EDGES,), 0, N_NODES, dtype=jnp.int32)
        dst = jax.random.randint(k3, (N_EDGES,), 0, N_NODES, dtype=jnp.int32)
        s = 1.0 / np.sqrt(D)
        theta_w = jax.random.uniform(k4, (D, D), jnp.float32, -s, s)
        theta_b = jnp.zeros((D,), jnp.float32)
        phi_w = jax.random.uniform(k5, (D, D), jnp.float32, -s, s)
        phi_b = jnp.zeros((D,), jnp.float32)
        return {'x': x, 'src': src, 'dst': dst, 'theta_w': theta_w, 'theta_b': theta_b, 'phi_w': phi_w, 'phi_b': phi_b}
    _L0_gnn_all = _L0_gnn_setup()
    _L0_gnn_in = {k: v for k, v in _L0_gnn_all.items() if k in ('theta_w', 'theta_b', 'phi_w', 'phi_b')}
    del _L0_gnn_all
    return {'x': x, 'src': src, 'dst': dst, 'L0_gnn_theta_w': _L0_gnn_in['theta_w'], 'L0_gnn_theta_b': _L0_gnn_in['theta_b'], 'L0_gnn_phi_w': _L0_gnn_in['phi_w'], 'L0_gnn_phi_b': _L0_gnn_in['phi_b']}

def reference(x, src, dst, L0_gnn_theta_w, L0_gnn_theta_b, L0_gnn_phi_w, L0_gnn_phi_b):
    import jax
    import jax.numpy as jnp

    def _L0_gnn_ref(x, src, dst, theta_w, theta_b, phi_w, phi_b):
        import jax, jax.numpy as jnp
        import numpy as np
        N_NODES = 1250
        N_EDGES = 40000
        D = 256
        x_src = x[src]
        x_dst = x[dst]
        theta_x = (x_dst - x_src) @ theta_w.T + theta_b
        phi_x = x_src @ phi_w.T + phi_b
        e = jax.nn.relu(theta_x + phi_x)
        out = jax.ops.segment_max(e, dst, num_segments=x.shape[0])
        return jnp.where(jnp.isfinite(out), out, 0.0)
    x = _layernorm(x + _L0_gnn_ref(x, src, dst, L0_gnn_theta_w, L0_gnn_theta_b, L0_gnn_phi_w, L0_gnn_phi_b), axis=-1)
    return x

_drawn_inputs = setup_inputs


def setup_inputs(seed=0):
    import zlib

    import numpy as np

    out = dict(_drawn_inputs(seed))
    spreads = {'L0_gnn_theta_b': (0.0, 0.1), 'L0_gnn_phi_b': (0.0, 0.1)}
    factors = {}
    for name, (base, spread) in spreads.items():
        noise = np.random.default_rng([zlib.crc32(name.encode()), seed]).standard_normal(out[name].shape)
        drawn = base * np.exp(spread * noise) if base else spread * noise
        out[name] = jnp.asarray(drawn.astype(out[name].dtype))
    for name, factor in factors.items():
        out[name] = (out[name] * factor).astype(out[name].dtype)
    return out
```

```python
from contextlib import ExitStack

import concourse.bass as bass
from concourse import mybir

P = 128
ALU = mybir.AluOpType
ACT = mybir.ActivationFunctionType
F32 = mybir.dt.float32
BF16 = mybir.dt.bfloat16
I32 = mybir.dt.int32
AX_X = mybir.AxisListType.X
FLT_MAX = 3.4028234663852886e38
EPS = 1e-5

CHUNK = 7
GROUPS = (5, 4, 4, 4)
QUARTER = 4


def build(nc, x, xt, src, dst, theta_t, phi_t, theta_b, phi_b, out):
    N, D = x.shape
    E = src.shape[0]
    NT = (N + P - 1) // P
    KC = D // P
    STEPS = (E + P - 1) // P
    U = sum(GROUPS)
    NG = len(GROUPS)
    START = [sum(GROUPS[:g]) for g in range(NG)]
    TURNS = STEPS // U
    FULL_P = E // STEPS
    REST = E - FULL_P * STEPS
    MIX = 3
    EARLY = MIX * U
    CONVERT = 3
    BESIDE = EARLY // CONVERT
    COUNT = (TURNS - BESIDE - MIX) // 2
    LAST = TURNS - BESIDE - 3 * MIX - COUNT
    MIX_AT, COUNT_AT, LAST_AT = BESIDE, BESIDE + 3 * MIX, BESIDE + 3 * MIX + COUNT
    GATHERED = TURNS - MIX
    A_BESIDE, A_MIX = 2, 3
    A_LOOP = A_BESIDE * BESIDE + A_MIX * MIX
    CHUNKS = NT // CHUNK
    assert STEPS % U == 0 and NT % CHUNK == 0 and CHUNKS % 2 == 1 and D % P == 0 and FULL_P == P - 1
    assert BESIDE + MIX + 2 * COUNT == TURNS and LAST > 0 and NT - CHUNK <= A_LOOP <= NT
    ACC0 = (0, 4, 0, 4)
    OUT_TURNS = (NT - 1) // (4 * QUARTER)
    assert OUT_TURNS * 4 * QUARTER == NT - 1
    LAST_ROWS = N - (NT - 1) * P
    FAR = 1 << 20

    with ExitStack() as ctx:
        def sb(name, shape, dt=F32):
            return ctx.enter_context(nc.sbuf_tensor(name, shape, dt))

        def ps(name, shape):
            return ctx.enter_context(nc.psum_tensor(name, shape, F32))

        def sem(name):
            return ctx.enter_context(nc.semaphore(name))

        b_table = nc.dram_tensor("b_table", (NT * P, D), F32).ap()
        runmax = nc.dram_tensor("runmax", (P * STEPS, D), F32).ap()
        runmax_by_p = runmax.rearrange("(p k) d -> p k d", p=P)

        xt_sb = sb("xt_sb", [P, 2 * CHUNK, KC, P])
        theta_sb = sb("theta_sb", [P, KC, D])
        diff_sb = sb("diff_sb", [P, KC, D])
        bias = sb("bias", [P, D])
        bias2 = sb("bias2", [P, D])
        early = sb("early", [P, max(EARLY, NT), D])
        x_sb = early[:, 0:NT, :]
        a_sb = sb("a_sb", [P, NT, D])
        rows = sb("rows", [P, U, D])
        hist = sb("hist", [P, U, D])
        idx = sb("idx", [P, STEPS + 2 * U], I32)
        stage = sb("stage", [P, U], I32)
        reset = sb("reset", [P, STEPS])
        reset_now = sb("reset_now", [P, U])
        hi = sb("hi", [P, STEPS], BF16)
        lo = sb("lo", [P, STEPS], BF16)
        hot_hi = sb("hot_hi", [P, U, NT], BF16)
        hot_lo = sb("hot_lo", [P, U, P], BF16)
        conv_in = sb("conv_in", [P, CONVERT, D])
        conv_t = sb("conv_t", [P, KC, P])
        cols_i = sb("cols_i", [P, P], I32)
        part_i = sb("part_i", [P, 1], I32)
        cols = sb("cols", [P, P])
        cols_b = sb("cols_b", [P, P], BF16)
        part = sb("part", [P, 1])
        ident = sb("ident", [P, P])
        ones = sb("ones", [P, P])
        below = sb("below", [P, NT])
        zero_b = sb("zero_b", [P, P], BF16)
        small = sb("small", [P, 16])
        fix_row = sb("fix_row", [P, 1], I32)
        diag = sb("diag", [P, P])
        carry_on = sb("carry_on", [P, P])
        scanned = sb("scanned", [P, KC, P + 1])
        fix = sb("fix", [P, D])
        counts = sb("counts", [P, P])
        csum = sb("csum", [P, P])
        ends = sb("ends", [P, P])
        end_row = sb("end_row", [P, NT], I32)
        has = sb("has", [P, NT])
        stats = sb("stats", [P, 4 * QUARTER, 6])
        meanvar = sb("meanvar", [P, 4 * QUARTER, 2])
        sd = sb("sd", [P, 4 * QUARTER])
        eps = sb("eps", [P, 1])
        rstd = sb("rstd", [P, 4 * QUARTER])
        shift = sb("shift", [P, 4 * QUARTER])
        hist_flat = hist[:].rearrange("p u d -> p (u d)")
        dwin = hist_flat[:, 0:STEPS + 2].bitcast(I32)
        flag = hist_flat[:, 1000:1000 + STEPS]
        pos = hist_flat[:, 2000:2000 + STEPS]
        pos_i = hist_flat[:, 3000:3000 + STEPS].bitcast(I32)
        assert STEPS + 2 <= 1000 and (U - 1) * D >= 3000 + STEPS

        acc = ps("acc", [P, 8, D])
        ps_t = ps("ps_t", [P, 2, D])
        ps_b = ps("ps_b", [P, 2, D])
        ps_a = ps("ps_a", [P, 2, D])
        ps_h = ps("ps_h", [P, 2, D])
        b_psum = [acc[:, 0, :], acc[:, 2, :], acc[:, 4, :], acc[:, 6, :], ps_t[:, 0, :], ps_b[:, 0, :],
                  ps_a[:, 0, :]]
        assert len(b_psum) == CHUNK

        s_w = sem("weights_loaded")
        s_xt = [sem(f"xt_chunk_loaded{h}") for h in range(2)]
        s_at = [sem(f"xt_tile_loaded{j}") for j in range(A_MIX)]
        s_idx = sem("src_loaded")
        s_dst = sem("dst_loaded")
        s_bias = sem("bias_loaded")
        s_x = sem("x_loaded")
        s_iota = sem("iotas_made")
        s_diff = sem("diff_made")
        s_bmm = sem("b_tile_in_psum")
        s_bev = sem("b_tile_evacuated")
        s_bout = [sem(f"b_chunk_written{h}") for h in range(2)]
        s_prep = sem("prep_steps")
        s_pad = sem("pads_cleared")
        s_const = sem("constants_ready")
        s_flags = sem("flags_spread")
        s_xrows = sem("x_rows_gathered")
        s_cin = sem("conversion_staged")
        s_ct = sem("rows_transposed")
        s_cte = sem("transposed_rows_copied")
        s_cb = sem("rows_converted")
        s_cbe = sem("converted_rows_copied")
        s_amm = sem("a_tile_in_psum")
        s_aev = sem("a_tile_evacuated")
        s_stage = [sem(f"indices_staged{g}") for g in range(NG)]
        s_got = [sem(f"rows_gathered{g}") for g in range(NG)]
        s_reset = sem("resets_staged")
        s_fold = sem("steps_folded")
        s_copied = [sem(f"maxima_copied{g}") for g in range(NG)]
        s_hout = [sem(f"maxima_written{g}") for g in range(NG)]
        s_hot = sem("one_hots_made")
        s_hotused = sem("one_hots_used")
        s_csum = sem("counts_summed")
        s_before = sem("edges_before_tiles")
        s_ends = sem("last_edges_by_tile")
        s_turned = sem("last_edges_and_counts_turned")
        s_masked = sem("empty_nodes_masked")
        s_lastt = sem("last_maxima_transposed")
        s_scan = sem("partitions_scanned")
        s_carry = sem("carries_by_partition")
        s_fixin = sem("fix_rows_gathered")
        s_fixed = sem("fix_rows_ready")
        s_fixout = sem("fix_rows_written")
        s_end = [sem(f"end_rows_added{q}") for q in range(4)]
        s_o = sem("output_steps")
        s_var = sem("variances_ready")
        s_sd = sem("deviations_ready")
        s_scale = sem("scales_ready")
        s_norm = sem("tiles_normalised")
        s_out = [sem(f"output_written{q}") for q in range(4)]

        def a_tile(j):
            return CHUNK + j

        block = ctx.enter_context(nc.Block())

        @block.sync
        def _(sp):
            by_chunk = xt.rearrange("(c j) p k n -> c p j (k n)", j=CHUNK)
            xt_flat = xt_sb[:].rearrange("p j k n -> p j (k n)")
            table = b_table.rearrange("(c j p) d -> c p j d", j=CHUNK, p=P)

            def load(c, h):
                sp.dma_start(xt_flat[:, h * CHUNK:(h + 1) * CHUNK], by_chunk[c]).then_inc(s_xt[h], 16)

            def load_at(c, h):
                sp.dma_start(xt_flat[:, h * CHUNK:(h + 1) * CHUNK],
                             by_chunk[bass.ds(c, 1)].rearrange("a p j n -> p (a j) n")).then_inc(s_xt[h], 16)

            def store_at(c, h):
                sp.dma_start(table[bass.ds(c, 1)].rearrange("a p j d -> p (a j) d"),
                             rows[:, h * CHUNK:(h + 1) * CHUNK, :]).then_inc(s_bout[h], 16)

            sp.dma_start(theta_sb[:], theta_t.rearrange("(c p) d -> p c d", p=P)).then_inc(s_w, 16)
            load(0, 0)
            sp.dma_start(diff_sb[:], phi_t.rearrange("(c p) d -> p c d", p=P)).then_inc(s_w, 16)
            load(1, 1)
            sp.wait_ge(s_bmm, CHUNK)
            load(2, 0)
            sp.wait_ge(s_bev, CHUNK)
            sp.dma_start(table[0], rows[:, 0:CHUNK, :]).then_inc(s_bout[0], 16)
            with sp.Fori(1, (CHUNKS - 1) // 2) as m:
                sp.wait_ge(s_bmm, m * 2 * CHUNK)
                load_at(m * 2 + 1, 1)
                sp.wait_ge(s_bev, m * 2 * CHUNK)
                store_at(m * 2 - 1, 1)
                sp.wait_ge(s_bmm, m * 2 * CHUNK + CHUNK)
                load_at(m * 2 + 2, 0)
                sp.wait_ge(s_bev, m * 2 * CHUNK + CHUNK)
                store_at(m * 2, 0)
            sp.wait_ge(s_bev, (CHUNKS - 1) * CHUNK)
            sp.dma_start(table[CHUNKS - 2], rows[:, CHUNK:2 * CHUNK, :]).then_inc(s_bout[1], 16)
            sp.wait_ge(s_bmm, (CHUNKS - 1) * CHUNK)
            for j in range(A_MIX):
                t = j if j < A_BESIDE else A_BESIDE * BESIDE + j
                sp.dma_start(xt_flat[:, a_tile(j)], xt[t].rearrange("p k n -> p (k n)")).then_inc(s_at[j], 16)
            sp.wait_ge(s_bev, NT)
            sp.dma_start(table[CHUNKS - 1], rows[:, 0:CHUNK, :]).then_inc(s_bout[0], 16)

            def maxima_out(turn):
                for g, n in enumerate(GROUPS):
                    sp.wait_ge(s_copied[g], turn + 1)
                    sp.dma_start(runmax_by_p[:, bass.ds(turn * U + START[g], n), :],
                                 hist[:, START[g]:START[g] + n, :]).then_inc(s_hout[g], 16)

            def next_tiles(done, first, n):
                sp.wait_ge(s_amm, done)
                for j in range(n):
                    sp.dma_start(xt_flat[:, a_tile(j):a_tile(j) + 1],
                                 xt[bass.ds(first + j, 1)].rearrange("a p k n -> p a (k n)")
                                 ).then_inc(s_at[j], 16)

            A_PRE = NT - A_LOOP
            with sp.Fori(0, BESIDE) as i:
                maxima_out(i)
                next_tiles(i * A_BESIDE + (A_PRE + A_BESIDE), i * A_BESIDE + A_BESIDE, A_BESIDE)
            with sp.Fori(0, MIX) as i:
                maxima_out(i * 3 + MIX_AT)
                maxima_out(i * 3 + (MIX_AT + 1))
                maxima_out(i * 3 + (MIX_AT + 2))
                next_tiles(i * A_MIX + (A_PRE + A_BESIDE * BESIDE + A_MIX),
                           i * A_MIX + (A_BESIDE * BESIDE + A_MIX), A_MIX)
            sp.wait_ge(s_fold, COUNT_AT * U)
            full = x[0:(NT - 1) * P].rearrange("(t p) d -> p t d", p=P)
            sp.dma_start(x_sb[:, 0:NT - 1, :], full).then_inc(s_x, 16)
            sp.wait_ge(s_pad, 2)
            sp.dma_start(x_sb[0:LAST_ROWS, NT - 1, :], x[(NT - 1) * P:N]).then_inc(s_x, 16)
            with sp.Fori(COUNT_AT, TURNS) as turn:
                maxima_out(turn)

            out_tiles = out[0:(NT - 1) * P].rearrange("(t p) d -> p t d", p=P)
            with sp.Fori(0, OUT_TURNS) as c:
                for q in range(4):
                    sp.wait_ge(s_norm, c * 4 * QUARTER + (q + 1) * QUARTER)
                    sp.dma_start(out_tiles[:, bass.ds(c * 4 * QUARTER + q * QUARTER, QUARTER), :],
                                 hist[:, q * QUARTER:(q + 1) * QUARTER, :]).then_inc(s_out[q], 16)
            sp.wait_ge(s_norm, NT)
            sp.dma_start(out[(NT - 1) * P:N], hist[0:LAST_ROWS, U - 1, :]).then_inc(s_out[0], 16)
            sp.wait_ge(s_out[0], 16 * (OUT_TURNS + 1))
            for q in range(1, 4):
                sp.wait_ge(s_out[q], 16 * OUT_TURNS)

        @block.gpsimd
        def _(pool):
            nc.gpsimd.iota(cols_i[:], pattern=[[1, P]], base=0, channel_multiplier=0).then_inc(s_iota, 1)
            nc.gpsimd.iota(part_i[:], pattern=[[1, 1]], base=0, channel_multiplier=1).then_inc(s_iota, 1)
            nc.gpsimd.iota(pos_i, pattern=[[1, STEPS]], base=0, channel_multiplier=0).then_inc(s_iota, 1)
            pool.wait_ge(s_idx, 32)
            for m in range(MIX):
                for s in range(U):
                    k = (MIX_AT + 3 * m + 1) * U + s
                    pool.indirect_dma_start(
                        out=early[:, m * U + s, :], out_offset=None, in_=x,
                        in_offset=bass.IndirectOffsetOnAxis(ap=idx[:, k:k + 1], axis=0)
                    ).then_inc(s_xrows, 16)
            pool.wait_ge(s_bout[0], 16 * (CHUNKS + 1) // 2)
            pool.wait_ge(s_bout[1], 16 * (CHUNKS // 2))
            with pool.Fori(0, GATHERED) as i:
                for g, n in enumerate(GROUPS):
                    pool.wait_ge(s_stage[g], i + 1)
                    pool.nop(nofuse=True)
                    for s in range(START[g], START[g] + n):
                        pool.indirect_dma_start(
                            out=rows[:, s, :], out_offset=None, in_=b_table,
                            in_offset=bass.IndirectOffsetOnAxis(ap=stage[:, s:s + 1], axis=0)
                        ).then_inc(s_got[g], 16)
            for g in range(NG):
                pool.wait_ge(s_hout[g], 16 * TURNS)
            pool.wait_ge(s_masked, 1)
            pool.indirect_dma_start(
                out=fix[:], out_offset=None, in_=runmax,
                in_offset=bass.IndirectOffsetOnAxis(ap=fix_row[:], axis=0),
                bounds_check=E - 1, oob_is_err=False).then_inc(s_fixin, 16)
            pool.wait_ge(s_fixed, 1)
            pool.indirect_dma_start(
                out=runmax, out_offset=bass.IndirectOffsetOnAxis(ap=fix_row[:], axis=0), in_=fix[:],
                in_offset=None, bounds_check=E - 1, oob_is_err=False).then_inc(s_fixout, 16)
            pool.wait_ge(s_fixout, 16)
            for t in range(NT):
                turn, q = divmod(t // QUARTER, 4)
                if turn and t % QUARTER == 0:
                    pool.wait_ge(s_end[q], 16 * QUARTER * turn)
                pool.indirect_dma_start(
                    out=a_sb[:, t, :], out_offset=None, in_=runmax,
                    in_offset=bass.IndirectOffsetOnAxis(ap=end_row[:, t:t + 1], axis=0),
                    compute_op=ALU.add).then_inc(s_end[q], 16)

        @block.scalar
        def _(act):
            act.wait_ge(s_pad, 1)
            act.dma_start(idx[0:FULL_P, 0:STEPS],
                          src[0:FULL_P * STEPS].rearrange("(p k) -> p k", k=STEPS)).then_inc(s_idx, 16)
            act.dma_start(idx[FULL_P:P, 0:REST],
                          src[FULL_P * STEPS:E].rearrange("(p k) -> p k", p=1)).then_inc(s_idx, 16)
            act.dma_start(dwin[0:FULL_P, 1:STEPS + 1],
                          dst[0:FULL_P * STEPS].rearrange("(p k) -> p k", k=STEPS)).then_inc(s_dst, 16)
            act.dma_start(dwin[FULL_P:P, 1:REST + 1],
                          dst[FULL_P * STEPS:E].rearrange("(p k) -> p k", p=1)).then_inc(s_dst, 16)
            ends_of_runs = dst[0:FULL_P * STEPS].rearrange("(p k) -> p k", k=STEPS)
            with nc.allow_non_contiguous_dma(reason="one number per partition"):
                act.dma_start(dwin[1:P, 0:1], ends_of_runs[:, STEPS - 1:STEPS]).then_inc(s_dst, 16)
                starts = dst[STEPS:FULL_P * STEPS].rearrange("(p k) -> p k", k=STEPS)
                act.dma_start(dwin[0:FULL_P - 1, STEPS + 1:STEPS + 2], starts[:, 0:1]).then_inc(s_dst, 16)
                act.dma_start(dwin[FULL_P - 1:FULL_P, STEPS + 1:STEPS + 2],
                              dst[FULL_P * STEPS:FULL_P * STEPS + 1].rearrange("(p k) -> p k", p=1)
                              ).then_inc(s_dst, 16)
            act.dma_start(bias[:], theta_b.rearrange("(a d) -> a d", a=1).broadcast_to([P, D])).then_inc(s_bias, 16)
            act.dma_start(bias2[:], phi_b.rearrange("(a d) -> a d", a=1).broadcast_to([P, D])).then_inc(s_bias, 16)

            def evacuate(base, h):
                for j in range(CHUNK):
                    act.wait_ge(s_bmm, base + j + 1)
                    nc.scalar.copy(rows[:, h * CHUNK + j, :], b_psum[j]).then_inc(s_bev, 1)

            evacuate(0, 0)
            evacuate(CHUNK, 1)
            act.wait_ge(s_bout[0], 16)
            evacuate(2 * CHUNK, 0)
            with act.Fori(2, (CHUNKS - 1) // 2 + 1) as m:
                for h in (1, 0):
                    act.wait_ge(s_bout[h], m * 16 - 16 * h)
                    evacuate(m * 2 * CHUNK - h * CHUNK, h)
            act.wait_ge(s_const, 1)

            def maxima_copy(turn, g, first):
                act.wait_ge(s_fold, turn * U + (START[g] + GROUPS[g]))
                if not first:
                    act.wait_ge(s_hout[g], turn * 16)
                nc.scalar.copy(hist[:, START[g]:START[g] + GROUPS[g] - 1, :],
                               acc[:, ACC0[g]:ACC0[g] + GROUPS[g] - 1, :]).then_inc(s_copied[g], 1)

            def transposed(i, r):
                act.wait_ge(s_ct, i * CONVERT + (r + 1))
                nc.scalar.copy(conv_t[:].rearrange("p k n -> p (k n)"), ps_t[:, 0, :]).then_inc(s_cte, 1)

            def converted(i, r):
                act.wait_ge(s_cb, i * CONVERT + (r + 1))
                act.nop(nofuse=True)
                nc.scalar.copy(early[:, bass.ds(i * CONVERT + r, 1), :].rearrange("p a d -> p (a d)"),
                               ps_b[:, 0, :]).then_inc(s_cbe, 1)

            def beside(i, first):
                if first:
                    act.wait_ge(s_xrows, 16 * EARLY)
                else:
                    act.wait_ge(s_ct, i * CONVERT)
                    act.nop(nofuse=True)
                nc.scalar.copy(conv_in[:], early[:, bass.ds(i * CONVERT, CONVERT), :]).then_inc(s_cin, 1)
                for g in range(NG):
                    maxima_copy(i, g, first)
                    if g > 0:
                        converted(i, g - 1)
                    if g < CONVERT:
                        transposed(i, g)

            assert NG == CONVERT + 1
            beside(0, True)
            with act.Fori(1, BESIDE) as i:
                beside(i, False)
            with act.Fori(MIX_AT, TURNS) as turn:
                for g in range(NG):
                    maxima_copy(turn, g, False)
            for g in range(NG):
                act.wait_ge(s_hout[g], 16 * TURNS)

            def deviation(quarters, first, tiles):
                act.wait_ge(s_var, quarters + 1)
                these = slice(first, first + tiles)
                nc.scalar.activation(sd[:, these], meanvar[:, these, 1], ACT.Sqrt,
                                     bias=eps[:, 0:1]).then_inc(s_sd, 1)

            def normalise(quarters, first, tiles, slot):
                act.wait_ge(s_scale, quarters + 1)
                for j in range(tiles):
                    nc.scalar.activation(hist[:, slot + j, :], hist[:, slot + j, :], ACT.Identity,
                                         scale=rstd[:, first + j:first + j + 1],
                                         bias=shift[:, first + j:first + j + 1]).then_inc(s_norm, 1)

            with act.Fori(0, OUT_TURNS) as c:
                for q in range(4):
                    deviation(c * 4 + q, q * QUARTER, QUARTER)
                    normalise(c * 4 + q, q * QUARTER, QUARTER, q * QUARTER)
            deviation(4 * OUT_TURNS, 0, 1)
            normalise(4 * OUT_TURNS, 0, 1, U - 1)

        @block.tensor
        def _(pe):
            def table(base, h, first):
                for j in range(CHUNK):
                    if not first:
                        pe.wait_ge(s_bev, base - CHUNK + j + 1)
                    for k in range(KC):
                        mm = pe.matmul(b_psum[j], xt_sb[:, h * CHUNK + j, k, :], diff_sb[:, k, :],
                                       start=(k == 0), stop=(k == KC - 1))
                    mm.then_inc(s_bmm, 1)

            pe.wait_ge(s_diff, 1)
            pe.wait_ge(s_xt[0], 16)
            table(0, 0, True)
            with pe.Fori(1, (CHUNKS - 1) // 2 + 1) as m:
                for h in (1, 0):
                    pe.wait_ge(s_xt[h], m * 16 + 16 * (1 - h))
                    table(m * 2 * CHUNK - h * CHUNK, h, False)

            A_PRE = NT - A_LOOP

            def a_product(done, slot):
                pe.wait_ge(s_aev, done)
                for k in range(KC):
                    mm = pe.matmul(ps_a[:, 0, :], xt_sb[:, slot, k, :], theta_sb[:, k, :],
                                   start=(k == 0), stop=(k == KC - 1))
                mm.then_inc(s_amm, 1)

            pe.wait_ge(s_bev, NT)
            for t in range(A_LOOP, NT):
                k0 = t - A_LOOP
                if k0:
                    a_product(k0, t % CHUNK)
                else:
                    for k in range(KC):
                        mm = pe.matmul(ps_a[:, 0, :], xt_sb[:, t % CHUNK, k, :], theta_sb[:, k, :],
                                       start=(k == 0), stop=(k == KC - 1))
                    mm.then_inc(s_amm, 1)
            pe.wait_ge(s_const, 1)
            pe.matmul(ps_b[:, 0, 0:P], ones[:], diag[:], start=True, stop=True).then_inc(s_flags, 1)
            pe.matmul(ps_h[0:NT, 0, 0:P], zero_b[:, 0:NT], zero_b[:], start=True, stop=False,
                      skip_group_check=True)
            pe.wait_ge(s_const, 2)

            def count(share):
                pe.wait_ge(s_hot, share + 1)
                for s in range(U):
                    mm = pe.matmul(ps_h[0:NT, 0, 0:P], hot_hi[:, s, :], hot_lo[:, s, :],
                                   start=False, stop=False, skip_group_check=True)
                mm.then_inc(s_hotused, 1)

            def convert(i, r, first):
                if not first or r:
                    pe.wait_ge(s_cte, i * CONVERT + r)
                for k in range(KC):
                    mm = pe.transpose(ps_t[:, 0, k * P:(k + 1) * P], conv_in[:, r, k * P:(k + 1) * P], ident[:])
                mm.then_inc(s_ct, 1)
                if not first or r:
                    pe.wait_ge(s_cbe, i * CONVERT + r)
                pe.wait_ge(s_cte, i * CONVERT + (r + 1))
                for k in range(KC):
                    mm = pe.matmul(ps_b[:, 0, :], conv_t[:, k, :], diff_sb[:, k, :],
                                   start=(k == 0), stop=(k == KC - 1))
                mm.then_inc(s_cb, 1)

            def beside(i, first):
                for j in range(A_BESIDE):
                    pe.wait_ge(s_at[j], i * 16 + 16)
                    a_product(i * A_BESIDE + (A_PRE + j), a_tile(j))
                    if j == 0:
                        pe.wait_ge(s_cin, i + 1)
                        for r in range(CONVERT):
                            convert(i, r, first)
                count(i)

            beside(0, True)
            with pe.Fori(1, BESIDE) as i:
                beside(i, False)
            with pe.Fori(0, MIX) as i:
                for j in range(A_MIX):
                    pe.wait_ge(s_at[j], i * 16 + (16 + 16 * BESIDE * (j < A_BESIDE)))
                    a_product(i * A_MIX + (A_PRE + A_BESIDE * BESIDE + j), a_tile(j))
                count(i + BESIDE)
            with pe.Fori(BESIDE + MIX, TURNS) as share:
                count(share)
            pe.matmul(ps_h[0:NT, 0, 0:P], zero_b[:, 0:NT], zero_b[:], start=False, stop=True,
                      skip_group_check=True).then_inc(s_hotused, 1)
            pe.wait_ge(s_aev, NT)
            pe.wait_ge(s_csum, 1)
            pe.matmul(ps_a[0:NT, 0, 0:1], below[0:NT, :], csum[0:NT, P - 1:P], start=True,
                      stop=True).then_inc(s_before, 1)
            pe.wait_ge(s_ends, 2)
            pe.transpose(ps_a[:, 0, 0:NT], ends[0:NT, :], ident[0:NT, 0:NT]).then_inc(s_turned, 1)
            pe.transpose(ps_h[:, 0, 0:NT], counts[0:NT, :], ident[0:NT, 0:NT]).then_inc(s_turned, 1)
            pe.wait_ge(s_cbe, EARLY)
            pe.wait_ge(s_fold, STEPS)
            for k in range(KC):
                mm = pe.transpose(ps_t[:, 0, k * P:(k + 1) * P], hist[:, U - 1, k * P:(k + 1) * P], ident[:])
            mm.then_inc(s_lastt, 1)
            pe.wait_ge(s_scan, KC)
            for k in range(KC):
                mm = pe.transpose(ps_b[:, 0, k * P:(k + 1) * P], scanned[:, k, 0:P], ident[:])
            mm.then_inc(s_carry, 1)

        @block.vector
        def _(dve):
            prep = [0]

            def then(ins):
                prep[0] += 1
                ins.then_inc(s_prep, 1)
                dve.wait_ge(s_prep, prep[0])

            nc.vector.memset(idx[:], 0)
            nc.vector.memset(dwin, -1).then_inc(s_pad, 1)
            dve.wait_ge(s_w, 32)
            nc.vector.tensor_tensor(diff_sb[:], diff_sb[:], theta_sb[:], ALU.subtract).then_inc(s_diff, 1)
            dve.wait_ge(s_idx, 32)
            for g, n in enumerate(GROUPS):
                nc.vector.tensor_copy(stage[:, START[g]:START[g] + n],
                                      idx[:, START[g]:START[g] + n]).then_inc(s_stage[g], 1)
            dve.wait_ge(s_iota, 3)
            nc.vector.tensor_copy(cols[:], cols_i[:])
            nc.vector.tensor_copy(cols_b[:], cols_i[:])
            nc.vector.tensor_copy(pos, pos_i)
            then(nc.vector.tensor_copy(part[:], part_i[:]))
            nc.vector.tensor_scalar(ident[:], cols[:], part[:, 0:1], None, ALU.is_equal)
            nc.vector.tensor_scalar(below[:], cols[:, 0:NT], part[:, 0:1], None, ALU.is_gt)
            nc.vector.memset(ones[:], 1.0)
            nc.vector.memset(zero_b[:], 0.0)
            nc.vector.memset(fix[:], 0.0)
            nc.vector.memset(eps[:], EPS)
            nc.vector.memset(scanned[:, :, 0:1], 0.0)
            nc.vector.memset(hist[:, U - 1, :], -FLT_MAX)
            dve.wait_ge(s_dst, 80)
            cur, before, after = dwin[:, 1:STEPS + 1], dwin[:, 0:STEPS], dwin[:, 2:STEPS + 2]
            then(nc.vector.tensor_tensor(flag, cur, before, ALU.not_equal))
            nc.vector.tensor_copy(small[:, 0:1], flag[:, 0:1])
            nc.vector.tensor_scalar(reset[:], flag, -2.0, 1.0, ALU.mult, ALU.add)
            then(nc.vector.tensor_reduce(small[:, 1:2], flag, AX_X, ALU.max))
            nc.vector.tensor_scalar(reset[:], reset[:], FLT_MAX, None, ALU.mult)
            then(nc.vector.tensor_tensor(flag, cur, after, ALU.not_equal))
            then(nc.vector.scalar_tensor_tensor(flag, flag, -4096.0, pos, ALU.mult, ALU.add))
            then(nc.vector.tensor_reduce(small[:, 2:3], flag, AX_X, ALU.min))
            then(nc.vector.scalar_tensor_tensor(small[:, 3:4], small[:, 2:3], 0.0, small[:, 0:1],
                                                ALU.is_ge, ALU.add))
            then(nc.vector.tensor_scalar(small[:, 3:4], small[:, 3:4], float(FAR), 4096.0, ALU.mult, ALU.add))
            then(nc.vector.scalar_tensor_tensor(small[:, 4:5], part[:], float(STEPS), small[:, 3:4],
                                                ALU.mult, ALU.add))
            then(nc.vector.tensor_tensor(small[:, 5:6], small[:, 4:5], small[:, 2:3], ALU.add))
            nc.vector.tensor_copy(fix_row[:], small[:, 5:6])
            then(nc.vector.tensor_scalar(pos_i, cur, 7, None, ALU.arith_shift_right))
            nc.vector.tensor_copy(hi[:], pos_i)
            then(nc.vector.tensor_scalar(pos.bitcast(I32), cur, 127, None, ALU.bitwise_and))
            nc.vector.tensor_copy(lo[:], pos.bitcast(I32))
            then(nc.vector.tensor_scalar(diag[:], ident[:], small[:, 1:2], None, ALU.mult))
            dve.wait_ge(s_bias, 32)
            nc.vector.tensor_tensor(bias[:], bias[:], bias2[:], ALU.add).then_inc(s_const, 1)
            dve.wait_ge(s_const, 1)

            A_PRE = NT - A_LOOP

            def a_out(done, tile):
                dve.wait_ge(s_amm, done + 1)
                nc.vector.tensor_tensor(tile, ps_a[:, 0, :], bias[:], ALU.add).then_inc(s_aev, 1)

            for t in range(A_LOOP, NT):
                a_out(t - A_LOOP, a_sb[:, t, :])
            dve.wait_ge(s_flags, 1)
            then(nc.vector.tensor_scalar(carry_on[:], ps_b[:, 0, 0:P], -2.0, 1.0, ALU.mult, ALU.add))
            nc.vector.tensor_scalar(carry_on[:], carry_on[:], FLT_MAX, None, ALU.mult).then_inc(s_const, 1)

            def fold_turn(turn, gathered, ahead, first, early_at=None):
                if not first:
                    dve.wait_ge(s_fold, turn * U)
                nc.vector.tensor_copy(reset_now[:], reset[:, bass.ds(turn * U, U)]).then_inc(s_reset, 1)
                dve.wait_ge(s_reset, turn + 1)
                for g, n in enumerate(GROUPS):
                    if early_at is None:
                        dve.wait_ge(s_got[g], gathered * (16 * n) + 16 * n)
                    if g >= 2:
                        dve.wait_ge(s_copied[g - 2], turn + 1)
                    elif not first:
                        dve.wait_ge(s_copied[g + 2], turn)
                    for s in range(n):
                        k = START[g] + s
                        former = acc[:, ACC0[g] + s - 1, :] if s else hist[:, (k - 1) % U, :]
                        new = acc[:, ACC0[g] + s, :] if s < n - 1 else hist[:, k, :]
                        if early_at is None:
                            row = rows[:, k, :]
                        else:
                            row = early[:, bass.ds(early_at + k, 1), :].rearrange("p a d -> p (a d)")
                        if s == n - 1 and not first:
                            dve.wait_ge(s_hout[g], turn * 16)
                        if not first or k:
                            dve.wait_ge(s_fold, turn * U + k)
                        nc.vector.scalar_tensor_tensor(new, former, reset_now[:, k:k + 1], row,
                                                       ALU.min, ALU.max).then_inc(s_fold, 1)
                    if early_at is None:
                        dve.wait_ge(s_fold, turn * U + (START[g] + n))
                        nc.vector.tensor_copy(stage[:, START[g]:START[g] + n],
                                              idx[:, bass.ds((turn + ahead) * U + START[g], n)]
                                              ).then_inc(s_stage[g], 1)

            def one_hots(share, first):
                if not first:
                    dve.wait_ge(s_hotused, share)
                nc.vector.tensor_tensor(hot_hi[:], cols_b[:, 0:NT].unsqueeze(1).broadcast_to([P, U, NT]),
                                        hi[:, bass.ds(share * U, U)].unsqueeze(2).broadcast_to([P, U, NT]),
                                        ALU.is_equal)
                nc.vector.tensor_tensor(hot_lo[:], cols_b[:].unsqueeze(1).broadcast_to([P, U, P]),
                                        lo[:, bass.ds(share * U, U)].unsqueeze(2).broadcast_to([P, U, P]),
                                        ALU.is_equal).then_inc(s_hot, 1)

            def a_at(t):
                return a_sb[:, bass.ds(t, 1), :].rearrange("p a d -> p (a d)")

            def beside(i, first):
                fold_turn(i, i, 1, first)
                for j in range(A_BESIDE):
                    a_out(i * A_BESIDE + (A_PRE + j), a_at(i * A_BESIDE + j))
                    if j == 0:
                        one_hots(i, first)

            beside(0, True)
            with dve.Fori(1, BESIDE) as i:
                beside(i, False)
            with dve.Fori(0, MIX) as i:
                def a_mix(j):
                    a_out(i * A_MIX + (A_PRE + A_BESIDE * BESIDE + j), a_at(i * A_MIX + (A_BESIDE * BESIDE + j)))

                fold_turn(i * 3 + MIX_AT, i * 2 + BESIDE, 2, False)
                a_mix(0)
                dve.wait_ge(s_cbe, EARLY)
                fold_turn(i * 3 + (MIX_AT + 1), None, None, False, early_at=i * U)
                a_mix(1)
                one_hots(i + BESIDE, False)
                fold_turn(i * 3 + (MIX_AT + 2), i * 2 + (BESIDE + 1), 1, False)
                a_mix(2)
            nc.vector.memset(x_sb[96:P, NT - 1, :], 0.0).then_inc(s_pad, 1)
            with dve.Fori(0, COUNT) as i:
                fold_turn(i + COUNT_AT, i + (BESIDE + 2 * MIX), 1, False)
                for r in range(2):
                    one_hots(i * 2 + (BESIDE + MIX + r), False)

            dve.wait_ge(s_hotused, TURNS + 1)
            nc.vector.tensor_copy(counts[0:NT, :], ps_h[0:NT, 0, 0:P]).then_inc(s_ends, 1)
            nc.vector.tensor_tensor_scan(csum[0:NT, :], ones[0:NT, :], ps_h[0:NT, 0, 0:P], 0.0, ALU.mult,
                                         ALU.add).then_inc(s_csum, 1)
            dve.wait_ge(s_csum, 1)
            dve.wait_ge(s_before, 1)
            then(nc.vector.tensor_scalar(small[0:NT, 7:8], ps_a[0:NT, 0, 0:1], -1.0, None, ALU.add))
            nc.vector.tensor_scalar(ends[0:NT, :], csum[0:NT, :], small[0:NT, 7:8], 0.0, ALU.add,
                                    ALU.max).then_inc(s_ends, 1)
            dve.wait_ge(s_turned, 2)
            nc.vector.tensor_copy(end_row[:], ps_a[:, 0, 0:NT])
            then(nc.vector.tensor_scalar(has[:], ps_h[:, 0, 0:NT], 0.5, 2.0, ALU.is_gt, ALU.mult))
            then(nc.vector.tensor_scalar(has[:], has[:], 1.0, FLT_MAX, ALU.subtract, ALU.mult))

            def mask(t):
                nc.vector.tensor_scalar(a_at(t), a_at(t), has[:, bass.ds(t, 1)], None, ALU.min)

            MASKED = NT // LAST
            assert MASKED * LAST == NT
            with dve.Fori(0, LAST) as i:
                fold_turn(i + LAST_AT, i + (GATHERED - LAST), 1, False)
                for j in range(MASKED):
                    mask(i * MASKED + j)
            nc.vector.memset(small[:, 8:9], 0.0).then_inc(s_masked, 1)

            dve.wait_ge(s_lastt, 1)
            for k in range(KC):
                nc.vector.tensor_tensor_scan(scanned[:, k, 1:P + 1], carry_on[:], ps_t[:, 0, k * P:(k + 1) * P],
                                             -FLT_MAX, ALU.min, ALU.max).then_inc(s_scan, 1)
            dve.wait_ge(s_carry, 1)
            dve.wait_ge(s_fixin, 16)
            nc.vector.tensor_tensor(fix[:], fix[:], ps_b[:, 0, :], ALU.max).then_inc(s_fixed, 1)


            def drop_infinite(o, y, ready_sem, ready):
                dve.wait_ge(ready_sem, ready)
                nc.vector.scalar_tensor_tensor(y, y, FLT_MAX, y, ALU.is_le, ALU.mult).then_inc(s_o, 1)

            def statistics(o, y, xs, z, first, tiles, written_sem, written):
                if written_sem is not None:
                    dve.wait_ge(written_sem, written)
                dve.wait_ge(s_o, o)
                nc.vector.scalar_tensor_tensor(z, y, 0.0, xs, ALU.max, ALU.add).then_inc(s_o, 1)
                dve.wait_ge(s_o, o + 1)
                for j in range(tiles):
                    nc.vector.bn_stats(stats[:, first + j, :], z[:, j, :]).then_inc(s_o, 1)
                dve.wait_ge(s_o, o + 1 + tiles)
                dve.nop(nofuse=True)
                for j in range(tiles):
                    last = nc.vector.bn_aggr(meanvar[:, first + j, :], stats[:, first + j, :])
                    last.then_inc(s_o if j < tiles - 1 else s_var, 1)

            def scales(quarters, o, first, tiles):
                these = slice(first, first + tiles)
                dve.wait_ge(s_sd, quarters + 1)
                nc.vector.reciprocal(rstd[:, these], sd[:, these]).then_inc(s_o, 1)
                dve.wait_ge(s_o, o + 1)
                nc.vector.scalar_tensor_tensor(shift[:, these], meanvar[:, these, 0], -1.0, rstd[:, these],
                                               ALU.mult, ALU.mult).then_inc(s_scale, 1)

            PER_QUARTER = 2 + 2 * QUARTER
            dve.wait_ge(s_x, 32)
            for g in range(NG):
                dve.wait_ge(s_hout[g], 16 * TURNS)

            def out_turn(c, first):
                for q in range(4):
                    o = c * (4 * PER_QUARTER) + (q * PER_QUARTER - (q > 0))
                    tiles = bass.ds(c * 4 * QUARTER + q * QUARTER, QUARTER)
                    z = hist[:, q * QUARTER:(q + 1) * QUARTER, :]
                    drop_infinite(o, a_sb[:, tiles, :], s_end[q], (c + 1) * (16 * QUARTER))
                    if q:
                        scales(c * 4 + (q - 1), o + 1, (q - 1) * QUARTER, QUARTER)
                    statistics(o + (2 if q else 1), a_sb[:, tiles, :], x_sb[:, tiles, :], z, q * QUARTER, QUARTER,
                               None if first else s_out[q], c * 16)
                scales(c * 4 + 3, c * (4 * PER_QUARTER) + (4 * PER_QUARTER - 1), 3 * QUARTER, QUARTER)

            out_turn(0, True)
            with dve.Fori(1, OUT_TURNS) as c:
                out_turn(c, False)
            o = OUT_TURNS * 4 * PER_QUARTER
            drop_infinite(o, a_sb[:, NT - 1:NT, :], s_end[0], 16 * (QUARTER * OUT_TURNS + 1))
            statistics(o + 1, a_sb[:, NT - 1:NT, :], x_sb[:, NT - 1:NT, :], hist[:, U - 1:U, :], 0, 1, None, 0)
            scales(4 * OUT_TURNS, o + 3, 0, 1)


_INS = ["x", "xt", "src", "dst", "theta_t", "phi_t", "theta_b", "phi_b"]


def kernel(x, src, dst, L0_gnn_theta_w, L0_gnn_theta_b, L0_gnn_phi_w, L0_gnn_phi_b):
    import numpy as np
    import concourse.bacc as bacc
    from concourse.bass_utils import run_bass_kernel_spmd

    x = np.asarray(x)
    n, d = x.shape
    tiles = (n + P - 1) // P
    padded = np.zeros((tiles * P, d), x.dtype)
    padded[:n] = x
    xt = padded.reshape(tiles, P, d // P, P).transpose(0, 3, 2, 1)
    arrays = {
        "x": x, "xt": xt, "src": np.asarray(src), "dst": np.asarray(dst),
        "theta_t": np.asarray(L0_gnn_theta_w).T, "phi_t": np.asarray(L0_gnn_phi_w).T,
        "theta_b": np.asarray(L0_gnn_theta_b), "phi_b": np.asarray(L0_gnn_phi_b),
    }
    nc = bacc.Bacc("TRN2", target_bir_lowering=False, num_devices=1)
    ins, args = {}, []
    for name in _INS:
        a = np.ascontiguousarray(arrays[name])
        ins[f"in_{name}"] = a
        args.append(nc.dram_tensor(f"in_{name}", a.shape, mybir.dt.from_np(a.dtype), kind="ExternalInput").ap())
    out = nc.dram_tensor("out", (n, d), F32, kind="ExternalOutput").ap()
    build(nc, *args, out)
    r = run_bass_kernel_spmd(nc, [ins], core_ids=[0])
    return r.results[0]["out"]
```

```python
from contextlib import ExitStack

import concourse.bass as bass
from concourse import mybir

P = 128
ALU = mybir.AluOpType
ACT = mybir.ActivationFunctionType
F32 = mybir.dt.float32
BF16 = mybir.dt.bfloat16
I32 = mybir.dt.int32
AX_X = mybir.AxisListType.X
FLT_MAX = 3.4028234663852886e38
EPS = 1e-5

CHUNK = 7
PARTS = (4, 3)
GROUPS = (5, 4, 4, 4)
QUARTER = 4


def build(nc, x, xt, src, dst, theta_t, phi_t, theta_b, phi_b, out):
    N, D = x.shape
    E = src.shape[0]
    NT = (N + P - 1) // P
    KC = D // P
    STEPS = (E + P - 1) // P
    U = sum(GROUPS)
    NG = len(GROUPS)
    START = [sum(GROUPS[:g]) for g in range(NG)]
    TURNS = STEPS // U
    FULL_P = E // STEPS
    REST = E - FULL_P * STEPS
    MIX = 3
    MIX_TURNS = 5
    EARLY = MIX * U
    CONVERT = 3
    BESIDE = EARLY // CONVERT
    MIX_SHARES = 3
    COUNT = (TURNS - BESIDE - MIX_SHARES * MIX) // 2
    LAST = TURNS - BESIDE - MIX_TURNS * MIX - COUNT
    MIX_AT, COUNT_AT = BESIDE, BESIDE + MIX_TURNS * MIX
    LAST_AT = COUNT_AT + COUNT
    GATHERED = TURNS - MIX
    A_BESIDE, A_MIX = 2, 3
    A_LOOP = A_BESIDE * BESIDE + A_MIX * MIX
    CHUNKS = NT // CHUNK
    assert STEPS % U == 0 and NT % CHUNK == 0 and CHUNKS % 2 == 1 and D % P == 0 and FULL_P == P - 1
    assert BESIDE + MIX_SHARES * MIX + 2 * COUNT == TURNS and LAST > 1 and sum(PARTS) == CHUNK and NT - CHUNK <= A_LOOP <= NT
    X_TILES = 4
    X_LOADS = (NT - 1) // X_TILES
    assert X_LOADS * X_TILES == NT - 1 and X_LOADS < COUNT + LAST
    ACC0 = (0, 4, 0, 4)
    OUT_TURNS = (NT - 1) // (4 * QUARTER)
    assert OUT_TURNS * 4 * QUARTER == NT - 1
    LAST_ROWS = N - (NT - 1) * P
    FAR = 1 << 20

    with ExitStack() as ctx:
        def sb(name, shape, dt=F32):
            return ctx.enter_context(nc.sbuf_tensor(name, shape, dt))

        def ps(name, shape):
            return ctx.enter_context(nc.psum_tensor(name, shape, F32))

        def sem(name):
            return ctx.enter_context(nc.semaphore(name))

        b_table = nc.dram_tensor("b_table", (NT * P, D), F32).ap()
        runmax = nc.dram_tensor("runmax", (P * STEPS, D), F32).ap()
        runmax_by_p = runmax.rearrange("(p k) d -> p k d", p=P)

        xt_sb = sb("xt_sb", [P, 2 * CHUNK, KC, P])
        theta_sb = sb("theta_sb", [P, KC, D])
        diff_sb = sb("diff_sb", [P, KC, D])
        bias = sb("bias", [P, D])
        bias2 = sb("bias2", [P, D])
        early = sb("early", [P, max(EARLY, NT), D])
        x_sb = early[:, 0:NT, :]
        a_sb = sb("a_sb", [P, NT, D])
        rows = sb("rows", [P, U, D])
        hist = sb("hist", [P, U, D])
        idx = sb("idx", [P, STEPS + 2 * U], I32)
        stage = sb("stage", [P, U], I32)
        reset = sb("reset", [P, STEPS])
        reset_now = sb("reset_now", [P, U])
        hi = sb("hi", [P, STEPS], BF16)
        lo = sb("lo", [P, STEPS], BF16)
        hot_hi = sb("hot_hi", [P, U, NT], BF16)
        hot_lo = sb("hot_lo", [P, U, P], BF16)
        conv_in = sb("conv_in", [P, CONVERT, D])
        conv_t = sb("conv_t", [P, KC, P])
        cols_i = sb("cols_i", [P, P], I32)
        part_i = sb("part_i", [P, 1], I32)
        cols = sb("cols", [P, P])
        cols_b = sb("cols_b", [P, P], BF16)
        part = sb("part", [P, 1])
        ident = sb("ident", [P, P])
        ones = sb("ones", [P, P])
        below = sb("below", [P, NT])
        zero_b = sb("zero_b", [P, P], BF16)
        small = sb("small", [P, 16])
        fix_row = sb("fix_row", [P, 1], I32)
        diag = sb("diag", [P, P])
        carry_on = sb("carry_on", [P, P])
        scanned = sb("scanned", [P, KC, P + 1])
        fix = sb("fix", [P, D])
        counts = sb("counts", [P, P])
        csum = sb("csum", [P, P])
        ends = sb("ends", [P, P])
        end_row = sb("end_row", [P, NT], I32)
        has = sb("has", [P, NT])
        stats = sb("stats", [P, 4 * QUARTER, 6])
        meanvar = sb("meanvar", [P, 4 * QUARTER, 2])
        sd = sb("sd", [P, 4 * QUARTER])
        eps = sb("eps", [P, 1])
        rstd = sb("rstd", [P, 4 * QUARTER])
        shift = sb("shift", [P, 4 * QUARTER])
        hist_flat = hist[:].rearrange("p u d -> p (u d)")
        dwin = hist_flat[:, 0:STEPS + 2].bitcast(I32)
        flag = hist_flat[:, 1000:1000 + STEPS]
        pos = hist_flat[:, 2000:2000 + STEPS]
        pos_i = hist_flat[:, 3000:3000 + STEPS].bitcast(I32)
        assert STEPS + 2 <= 1000 and (U - 1) * D >= 3000 + STEPS

        acc = ps("acc", [P, 8, D])
        ps_t = ps("ps_t", [P, 2, D])
        ps_b = ps("ps_b", [P, 2, D])
        ps_a = ps("ps_a", [P, 2, D])
        ps_h = ps("ps_h", [P, 2, D])
        b_psum = [acc[:, 0, :], acc[:, 2, :], acc[:, 4, :], acc[:, 6, :], ps_t[:, 0, :], ps_b[:, 0, :],
                  ps_a[:, 0, :]]
        assert len(b_psum) == CHUNK

        s_w = sem("weights_loaded")
        s_xt = [[sem(f"xt_chunk_loaded{h}_{part}") for part in range(2)] for h in range(2)]
        s_at = [sem(f"xt_tile_loaded{j}") for j in range(A_MIX)]
        s_idx = sem("src_loaded")
        s_dst = sem("dst_loaded")
        s_bias = sem("bias_loaded")
        s_x = sem("x_loaded")
        s_iota = sem("iotas_made")
        s_diff = sem("diff_made")
        s_bmm = sem("b_tile_in_psum")
        s_bev = sem("b_tile_evacuated")
        s_bout = [sem(f"b_chunk_written{h}") for h in range(2)]
        s_prep = sem("prep_steps")
        s_pad = sem("pads_cleared")
        s_const = sem("constants_ready")
        s_flags = sem("flags_spread")
        s_xrows = sem("x_rows_gathered")
        s_cin = sem("conversion_staged")
        s_ct = sem("rows_transposed")
        s_cte = sem("transposed_rows_copied")
        s_cb = sem("rows_converted")
        s_cbe = sem("converted_rows_copied")
        s_amm = sem("a_tile_in_psum")
        s_aev = sem("a_tile_evacuated")
        s_stage = [sem(f"indices_staged{g}") for g in range(NG)]
        s_got = [sem(f"rows_gathered{g}") for g in range(NG)]
        s_reset = sem("resets_staged")
        s_fold = sem("steps_folded")
        s_copied = [sem(f"maxima_copied{g}") for g in range(NG)]
        s_hout = [sem(f"maxima_written{g}") for g in range(NG)]
        s_hot = sem("one_hots_made")
        s_hotused = sem("one_hots_used")
        s_csum = sem("counts_summed")
        s_before = sem("edges_before_tiles")
        s_ends = sem("last_edges_by_tile")
        s_turned = sem("last_edges_and_counts_turned")
        s_masked = sem("empty_nodes_masked")
        s_lastt = sem("last_maxima_transposed")
        s_scan = sem("partitions_scanned")
        s_carry = sem("carries_by_partition")
        s_fixin = sem("fix_rows_gathered")
        s_fixed = sem("fix_rows_ready")
        s_fixout = sem("fix_rows_written")
        s_end = [sem(f"end_rows_added{q}") for q in range(4)]
        s_o = sem("output_steps")
        s_var = sem("variances_ready")
        s_sd = sem("deviations_ready")
        s_scale = sem("scales_ready")
        s_norm = sem("tiles_normalised")
        s_out = [sem(f"output_written{q}") for q in range(4)]

        def a_tile(j):
            return CHUNK + j

        block = ctx.enter_context(nc.Block())

        @block.sync
        def _(sp):
            by_chunk = xt.rearrange("(c j) p k n -> c p j (k n)", j=CHUNK)
            xt_flat = xt_sb[:].rearrange("p j k n -> p j (k n)")
            table = b_table.rearrange("(c j p) d -> c p j d", j=CHUNK, p=P)

            def tiles_of(part):
                return slice(PARTS[0] * part, PARTS[0] + PARTS[1] * part)

            def load(c, h, part):
                at = tiles_of(part)
                sp.dma_start(xt_flat[:, h * CHUNK + at.start:h * CHUNK + at.stop],
                             by_chunk[c][:, at]).then_inc(s_xt[h][part], 16)

            def load_at(c, h, part):
                at = tiles_of(part)
                sp.dma_start(xt_flat[:, h * CHUNK + at.start:h * CHUNK + at.stop],
                             by_chunk[bass.ds(c, 1), :, at].rearrange("a p j n -> p (a j) n")
                             ).then_inc(s_xt[h][part], 16)

            def store_at(c, h):
                sp.dma_start(table[bass.ds(c, 1)].rearrange("a p j d -> p (a j) d"),
                             rows[:, h * CHUNK:(h + 1) * CHUNK, :]).then_inc(s_bout[h], 16)

            sp.dma_start(theta_sb[:], theta_t.rearrange("(c p) d -> p c d", p=P)).then_inc(s_w, 16)
            sp.dma_start(diff_sb[:], phi_t.rearrange("(c p) d -> p c d", p=P)).then_inc(s_w, 16)
            sp.wait_ge(s_pad, 1)
            sp.dma_start(idx[0:FULL_P, 0:STEPS],
                         src[0:FULL_P * STEPS].rearrange("(p k) -> p k", k=STEPS)).then_inc(s_idx, 16)
            sp.dma_start(idx[FULL_P:P, 0:REST],
                         src[FULL_P * STEPS:E].rearrange("(p k) -> p k", p=1)).then_inc(s_idx, 16)
            for c in range(2):
                for part in range(2):
                    load(c, c, part)
            sp.wait_ge(s_bmm, PARTS[0])
            load(2, 0, 0)
            sp.wait_ge(s_bmm, CHUNK)
            load(2, 0, 1)
            sp.wait_ge(s_bev, CHUNK)
            sp.dma_start(table[0], rows[:, 0:CHUNK, :]).then_inc(s_bout[0], 16)
            with sp.Fori(1, (CHUNKS - 1) // 2) as m:
                for h in (1, 0):
                    before = m * 2 * CHUNK - CHUNK * h
                    sp.wait_ge(s_bmm, before + PARTS[0])
                    load_at(m * 2 + (2 - h), h, 0)
                    sp.wait_ge(s_bmm, before + CHUNK)
                    load_at(m * 2 + (2 - h), h, 1)
                    sp.wait_ge(s_bev, before + CHUNK)
                    store_at(m * 2 - h, h)
            sp.wait_ge(s_bev, (CHUNKS - 1) * CHUNK)
            sp.dma_start(table[CHUNKS - 2], rows[:, CHUNK:2 * CHUNK, :]).then_inc(s_bout[1], 16)
            sp.wait_ge(s_bmm, (CHUNKS - 1) * CHUNK)
            for j in range(A_MIX):
                t = j if j < A_BESIDE else A_BESIDE * BESIDE + j
                sp.dma_start(xt_flat[:, a_tile(j)], xt[t].rearrange("p k n -> p (k n)")).then_inc(s_at[j], 16)
            sp.wait_ge(s_bev, NT)
            sp.dma_start(table[CHUNKS - 1], rows[:, 0:CHUNK, :]).then_inc(s_bout[0], 16)

            def maxima_out(turn):
                for g, n in enumerate(GROUPS):
                    sp.wait_ge(s_copied[g], turn + 1)
                    sp.dma_start(runmax_by_p[:, bass.ds(turn * U + START[g], n), :],
                                 hist[:, START[g]:START[g] + n, :]).then_inc(s_hout[g], 16)

            def next_tiles(done, first, n):
                sp.wait_ge(s_amm, done)
                for j in range(n):
                    sp.dma_start(xt_flat[:, a_tile(j):a_tile(j) + 1],
                                 xt[bass.ds(first + j, 1)].rearrange("a p k n -> p a (k n)")
                                 ).then_inc(s_at[j], 16)

            A_PRE = NT - A_LOOP
            with sp.Fori(0, BESIDE) as i:
                maxima_out(i)
                next_tiles(i * A_BESIDE + (A_PRE + A_BESIDE), i * A_BESIDE + A_BESIDE, A_BESIDE)
            with sp.Fori(0, MIX) as i:
                for q in range(MIX_TURNS):
                    maxima_out(i * MIX_TURNS + (MIX_AT + q))
                next_tiles(i * A_MIX + (A_PRE + A_BESIDE * BESIDE + A_MIX),
                           i * A_MIX + (A_BESIDE * BESIDE + A_MIX), A_MIX)
            sp.wait_ge(s_fold, COUNT_AT * U)
            sp.wait_ge(s_pad, 3)
            sp.dma_start(x_sb[0:LAST_ROWS, NT - 1, :], x[(NT - 1) * P:N]).then_inc(s_x, 16)
            by_load = x[0:(NT - 1) * P].rearrange("(c t p) d -> c p t d", p=P, t=X_TILES)
            with sp.Fori(0, X_LOADS) as i:
                maxima_out(i + COUNT_AT)
                sp.dma_start(x_sb[:, bass.ds(i * X_TILES, X_TILES), :],
                             by_load[bass.ds(i, 1)].rearrange("a p t d -> p (a t) d")).then_inc(s_x, 16)
            with sp.Fori(COUNT_AT + X_LOADS, TURNS) as turn:
                maxima_out(turn)

            out_tiles = out[0:(NT - 1) * P].rearrange("(t p) d -> p t d", p=P)
            with sp.Fori(0, OUT_TURNS) as c:
                for q in range(4):
                    sp.wait_ge(s_norm, c * 4 * QUARTER + (q + 1) * QUARTER)
                    sp.dma_start(out_tiles[:, bass.ds(c * 4 * QUARTER + q * QUARTER, QUARTER), :],
                                 hist[:, q * QUARTER:(q + 1) * QUARTER, :]).then_inc(s_out[q], 16)
            sp.wait_ge(s_norm, NT)
            sp.dma_start(out[(NT - 1) * P:N], hist[0:LAST_ROWS, U - 1, :]).then_inc(s_out[0], 16)
            sp.wait_ge(s_out[0], 16 * (OUT_TURNS + 1))
            for q in range(1, 4):
                sp.wait_ge(s_out[q], 16 * OUT_TURNS)

        @block.gpsimd
        def _(pool):
            nc.gpsimd.iota(cols_i[:], pattern=[[1, P]], base=0, channel_multiplier=0).then_inc(s_iota, 1)
            nc.gpsimd.iota(part_i[:], pattern=[[1, 1]], base=0, channel_multiplier=1).then_inc(s_iota, 1)
            nc.gpsimd.iota(pos_i, pattern=[[1, STEPS]], base=0, channel_multiplier=0).then_inc(s_iota, 1)
            pool.wait_ge(s_idx, 32)
            for m in range(MIX):
                for s in range(U):
                    k = (MIX_AT + MIX_TURNS * m + 1) * U + s
                    pool.indirect_dma_start(
                        out=early[:, m * U + s, :], out_offset=None, in_=x,
                        in_offset=bass.IndirectOffsetOnAxis(ap=idx[:, k:k + 1], axis=0)
                    ).then_inc(s_xrows, 16)
            pool.wait_ge(s_bout[0], 16 * (CHUNKS + 1) // 2)
            pool.wait_ge(s_bout[1], 16 * (CHUNKS // 2))
            with pool.Fori(0, GATHERED) as i:
                for g, n in enumerate(GROUPS):
                    pool.wait_ge(s_stage[g], i + 1)
                    pool.nop(nofuse=True)
                    for s in range(START[g], START[g] + n):
                        pool.indirect_dma_start(
                            out=rows[:, s, :], out_offset=None, in_=b_table,
                            in_offset=bass.IndirectOffsetOnAxis(ap=stage[:, s:s + 1], axis=0)
                        ).then_inc(s_got[g], 16)
            for g in range(NG):
                pool.wait_ge(s_hout[g], 16 * TURNS)
            pool.wait_ge(s_masked, 1)
            pool.indirect_dma_start(
                out=fix[:], out_offset=None, in_=runmax,
                in_offset=bass.IndirectOffsetOnAxis(ap=fix_row[:], axis=0),
                bounds_check=E - 1, oob_is_err=False).then_inc(s_fixin, 16)
            pool.wait_ge(s_fixed, 1)
            pool.indirect_dma_start(
                out=runmax, out_offset=bass.IndirectOffsetOnAxis(ap=fix_row[:], axis=0), in_=fix[:],
                in_offset=None, bounds_check=E - 1, oob_is_err=False).then_inc(s_fixout, 16)
            pool.wait_ge(s_fixout, 16)
            for t in range(NT):
                turn, q = divmod(t // QUARTER, 4)
                if turn and t % QUARTER == 0:
                    pool.wait_ge(s_end[q], 16 * QUARTER * turn)
                pool.indirect_dma_start(
                    out=a_sb[:, t, :], out_offset=None, in_=runmax,
                    in_offset=bass.IndirectOffsetOnAxis(ap=end_row[:, t:t + 1], axis=0),
                    compute_op=ALU.add).then_inc(s_end[q], 16)

        @block.scalar
        def _(act):
            act.wait_ge(s_pad, 2)
            act.wait_ge(s_w, 32)
            act.dma_start(dwin[0:FULL_P, 1:STEPS + 1],
                          dst[0:FULL_P * STEPS].rearrange("(p k) -> p k", k=STEPS)).then_inc(s_dst, 16)
            act.dma_start(dwin[FULL_P:P, 1:REST + 1],
                          dst[FULL_P * STEPS:E].rearrange("(p k) -> p k", p=1)).then_inc(s_dst, 16)
            ends_of_runs = dst[0:FULL_P * STEPS].rearrange("(p k) -> p k", k=STEPS)
            with nc.allow_non_contiguous_dma(reason="one number per partition"):
                act.dma_start(dwin[1:P, 0:1], ends_of_runs[:, STEPS - 1:STEPS]).then_inc(s_dst, 16)
                starts = dst[STEPS:FULL_P * STEPS].rearrange("(p k) -> p k", k=STEPS)
                act.dma_start(dwin[0:FULL_P - 1, STEPS + 1:STEPS + 2], starts[:, 0:1]).then_inc(s_dst, 16)
                act.dma_start(dwin[FULL_P - 1:FULL_P, STEPS + 1:STEPS + 2],
                              dst[FULL_P * STEPS:FULL_P * STEPS + 1].rearrange("(p k) -> p k", p=1)
                              ).then_inc(s_dst, 16)
            act.dma_start(bias[:], theta_b.rearrange("(a d) -> a d", a=1).broadcast_to([P, D])).then_inc(s_bias, 16)
            act.dma_start(bias2[:], phi_b.rearrange("(a d) -> a d", a=1).broadcast_to([P, D])).then_inc(s_bias, 16)

            def evacuate(base, h):
                for j in range(CHUNK):
                    act.wait_ge(s_bmm, base + j + 1)
                    nc.scalar.copy(rows[:, h * CHUNK + j, :], b_psum[j]).then_inc(s_bev, 1)

            evacuate(0, 0)
            evacuate(CHUNK, 1)
            act.wait_ge(s_bout[0], 16)
            evacuate(2 * CHUNK, 0)
            with act.Fori(2, (CHUNKS - 1) // 2 + 1) as m:
                for h in (1, 0):
                    act.wait_ge(s_bout[h], m * 16 - 16 * h)
                    evacuate(m * 2 * CHUNK - h * CHUNK, h)
            act.wait_ge(s_const, 1)

            def maxima_copy(turn, g, first):
                act.wait_ge(s_fold, turn * U + (START[g] + GROUPS[g]))
                if not first:
                    act.wait_ge(s_hout[g], turn * 16)
                nc.scalar.copy(hist[:, START[g]:START[g] + GROUPS[g] - 1, :],
                               acc[:, ACC0[g]:ACC0[g] + GROUPS[g] - 1, :]).then_inc(s_copied[g], 1)

            def transposed(i, r):
                act.wait_ge(s_ct, i * CONVERT + (r + 1))
                nc.scalar.copy(conv_t[:].rearrange("p k n -> p (k n)"), ps_t[:, 0, :]).then_inc(s_cte, 1)

            def converted(i, r):
                act.wait_ge(s_cb, i * CONVERT + (r + 1))
                act.nop(nofuse=True)
                nc.scalar.copy(early[:, bass.ds(i * CONVERT + r, 1), :].rearrange("p a d -> p (a d)"),
                               ps_b[:, 0, :]).then_inc(s_cbe, 1)

            def beside(i, first):
                if first:
                    act.wait_ge(s_xrows, 16 * EARLY)
                else:
                    act.wait_ge(s_ct, i * CONVERT)
                    act.nop(nofuse=True)
                nc.scalar.copy(conv_in[:], early[:, bass.ds(i * CONVERT, CONVERT), :]).then_inc(s_cin, 1)
                for g in range(NG):
                    maxima_copy(i, g, first)
                    if g > 0:
                        converted(i, g - 1)
                    if g < CONVERT:
                        transposed(i, g)

            assert NG == CONVERT + 1
            beside(0, True)
            with act.Fori(1, BESIDE) as i:
                beside(i, False)
            with act.Fori(MIX_AT, TURNS) as turn:
                for g in range(NG):
                    maxima_copy(turn, g, False)
            for g in range(NG):
                act.wait_ge(s_hout[g], 16 * TURNS)

            def deviation(quarters, first, tiles):
                act.wait_ge(s_var, quarters + 1)
                these = slice(first, first + tiles)
                nc.scalar.activation(sd[:, these], meanvar[:, these, 1], ACT.Sqrt,
                                     bias=eps[:, 0:1]).then_inc(s_sd, 1)

            def normalise(quarters, first, tiles, slot):
                act.wait_ge(s_scale, quarters + 1)
                for j in range(tiles):
                    nc.scalar.activation(hist[:, slot + j, :], hist[:, slot + j, :], ACT.Identity,
                                         scale=rstd[:, first + j:first + j + 1],
                                         bias=shift[:, first + j:first + j + 1]).then_inc(s_norm, 1)

            with act.Fori(0, OUT_TURNS) as c:
                for q in range(4):
                    deviation(c * 4 + q, q * QUARTER, QUARTER)
                    normalise(c * 4 + q, q * QUARTER, QUARTER, q * QUARTER)
            deviation(4 * OUT_TURNS, 0, 1)
            normalise(4 * OUT_TURNS, 0, 1, U - 1)

        @block.tensor
        def _(pe):
            def table(base, h, loaded, first):
                for j in range(CHUNK):
                    if j in (0, PARTS[0]):
                        pe.wait_ge(s_xt[h][j > 0], loaded)
                    if not first:
                        pe.wait_ge(s_bev, base - CHUNK + j + 1)
                    for k in range(KC):
                        mm = pe.matmul(b_psum[j], xt_sb[:, h * CHUNK + j, k, :], diff_sb[:, k, :],
                                       start=(k == 0), stop=(k == KC - 1))
                    mm.then_inc(s_bmm, 1)

            pe.wait_ge(s_diff, 1)
            table(0, 0, 16, True)
            with pe.Fori(1, (CHUNKS - 1) // 2 + 1) as m:
                for h in (1, 0):
                    table(m * 2 * CHUNK - h * CHUNK, h, m * 16 + 16 * (1 - h), False)

            A_PRE = NT - A_LOOP

            def a_product(done, slot):
                pe.wait_ge(s_aev, done)
                for k in range(KC):
                    mm = pe.matmul(ps_a[:, 0, :], xt_sb[:, slot, k, :], theta_sb[:, k, :],
                                   start=(k == 0), stop=(k == KC - 1))
                mm.then_inc(s_amm, 1)

            pe.wait_ge(s_bev, NT)
            for t in range(A_LOOP, NT):
                k0 = t - A_LOOP
                if k0:
                    a_product(k0, t % CHUNK)
                else:
                    for k in range(KC):
                        mm = pe.matmul(ps_a[:, 0, :], xt_sb[:, t % CHUNK, k, :], theta_sb[:, k, :],
                                       start=(k == 0), stop=(k == KC - 1))
                    mm.then_inc(s_amm, 1)
            pe.wait_ge(s_const, 1)
            pe.matmul(ps_b[:, 0, 0:P], ones[:], diag[:], start=True, stop=True).then_inc(s_flags, 1)
            pe.matmul(ps_h[0:NT, 0, 0:P], zero_b[:, 0:NT], zero_b[:], start=True, stop=False,
                      skip_group_check=True)
            pe.wait_ge(s_const, 2)

            def count(share):
                pe.wait_ge(s_hot, share + 1)
                for s in range(U):
                    mm = pe.matmul(ps_h[0:NT, 0, 0:P], hot_hi[:, s, :], hot_lo[:, s, :],
                                   start=False, stop=False, skip_group_check=True)
                mm.then_inc(s_hotused, 1)

            def convert(i, r, first):
                if not first or r:
                    pe.wait_ge(s_cte, i * CONVERT + r)
                for k in range(KC):
                    mm = pe.transpose(ps_t[:, 0, k * P:(k + 1) * P], conv_in[:, r, k * P:(k + 1) * P], ident[:])
                mm.then_inc(s_ct, 1)
                if not first or r:
                    pe.wait_ge(s_cbe, i * CONVERT + r)
                pe.wait_ge(s_cte, i * CONVERT + (r + 1))
                for k in range(KC):
                    mm = pe.matmul(ps_b[:, 0, :], conv_t[:, k, :], diff_sb[:, k, :],
                                   start=(k == 0), stop=(k == KC - 1))
                mm.then_inc(s_cb, 1)

            def beside(i, first):
                for j in range(A_BESIDE):
                    pe.wait_ge(s_at[j], i * 16 + 16)
                    a_product(i * A_BESIDE + (A_PRE + j), a_tile(j))
                    if j == 0:
                        pe.wait_ge(s_cin, i + 1)
                        for r in range(CONVERT):
                            convert(i, r, first)
                count(i)

            beside(0, True)
            with pe.Fori(1, BESIDE) as i:
                beside(i, False)
            with pe.Fori(0, MIX) as i:
                for j in range(A_MIX):
                    pe.wait_ge(s_at[j], i * 16 + (16 + 16 * BESIDE * (j < A_BESIDE)))
                    a_product(i * A_MIX + (A_PRE + A_BESIDE * BESIDE + j), a_tile(j))
                    count(i * MIX_SHARES + (BESIDE + j))
            with pe.Fori(BESIDE + MIX_SHARES * MIX, TURNS) as share:
                count(share)
            pe.matmul(ps_h[0:NT, 0, 0:P], zero_b[:, 0:NT], zero_b[:], start=False, stop=True,
                      skip_group_check=True).then_inc(s_hotused, 1)
            pe.wait_ge(s_aev, NT)
            pe.wait_ge(s_csum, 1)
            pe.matmul(ps_a[0:NT, 0, 0:1], below[0:NT, :], csum[0:NT, P - 1:P], start=True,
                      stop=True).then_inc(s_before, 1)
            pe.wait_ge(s_ends, 2)
            pe.transpose(ps_a[:, 0, 0:NT], ends[0:NT, :], ident[0:NT, 0:NT]).then_inc(s_turned, 1)
            pe.transpose(ps_h[:, 0, 0:NT], counts[0:NT, :], ident[0:NT, 0:NT]).then_inc(s_turned, 1)
            pe.wait_ge(s_cbe, EARLY)
            pe.wait_ge(s_fold, STEPS)
            for k in range(KC):
                mm = pe.transpose(ps_t[:, 0, k * P:(k + 1) * P], hist[:, U - 1, k * P:(k + 1) * P], ident[:])
            mm.then_inc(s_lastt, 1)
            pe.wait_ge(s_scan, KC)
            for k in range(KC):
                mm = pe.transpose(ps_b[:, 0, k * P:(k + 1) * P], scanned[:, k, 0:P], ident[:])
            mm.then_inc(s_carry, 1)

        @block.vector
        def _(dve):
            prep = [0]

            def then(ins):
                prep[0] += 1
                ins.then_inc(s_prep, 1)
                dve.wait_ge(s_prep, prep[0])

            nc.vector.memset(idx[96:P, REST:STEPS], 0)
            nc.vector.memset(idx[:, STEPS:], 0).then_inc(s_pad, 1)
            nc.vector.memset(dwin[96:P, REST:STEPS + 1], -1)
            nc.vector.memset(dwin[:, 0:1], -1)
            nc.vector.memset(dwin[:, STEPS + 1:STEPS + 2], -1).then_inc(s_pad, 1)
            dve.wait_ge(s_w, 32)
            nc.vector.tensor_tensor(diff_sb[:], diff_sb[:], theta_sb[:], ALU.subtract).then_inc(s_diff, 1)
            dve.wait_ge(s_idx, 32)
            for g, n in enumerate(GROUPS):
                nc.vector.tensor_copy(stage[:, START[g]:START[g] + n],
                                      idx[:, START[g]:START[g] + n]).then_inc(s_stage[g], 1)
            dve.wait_ge(s_iota, 3)
            nc.vector.tensor_copy(cols[:], cols_i[:])
            nc.vector.tensor_copy(cols_b[:], cols_i[:])
            nc.vector.tensor_copy(pos, pos_i)
            then(nc.vector.tensor_copy(part[:], part_i[:]))
            nc.vector.tensor_scalar(ident[:], cols[:], part[:, 0:1], None, ALU.is_equal)
            nc.vector.tensor_scalar(below[:], cols[:, 0:NT], part[:, 0:1], None, ALU.is_gt)
            nc.vector.memset(ones[:], 1.0)
            nc.vector.memset(zero_b[:], 0.0)
            nc.vector.memset(fix[:], 0.0)
            nc.vector.memset(eps[:], EPS)
            nc.vector.memset(scanned[:, :, 0:1], 0.0)
            nc.vector.memset(hist[:, U - 1, :], -FLT_MAX)
            dve.wait_ge(s_dst, 80)
            cur, before, after = dwin[:, 1:STEPS + 1], dwin[:, 0:STEPS], dwin[:, 2:STEPS + 2]
            then(nc.vector.tensor_tensor(flag, cur, before, ALU.not_equal))
            nc.vector.tensor_copy(small[:, 0:1], flag[:, 0:1])
            nc.vector.tensor_scalar(reset[:], flag, -2.0, 1.0, ALU.mult, ALU.add)
            then(nc.vector.tensor_reduce(small[:, 1:2], flag, AX_X, ALU.max))
            nc.vector.tensor_scalar(reset[:], reset[:], FLT_MAX, None, ALU.mult)
            then(nc.vector.tensor_tensor(flag, cur, after, ALU.not_equal))
            then(nc.vector.scalar_tensor_tensor(flag, flag, -4096.0, pos, ALU.mult, ALU.add))
            then(nc.vector.tensor_reduce(small[:, 2:3], flag, AX_X, ALU.min))
            then(nc.vector.scalar_tensor_tensor(small[:, 3:4], small[:, 2:3], 0.0, small[:, 0:1],
                                                ALU.is_ge, ALU.add))
            then(nc.vector.tensor_scalar(small[:, 3:4], small[:, 3:4], float(FAR), 4096.0, ALU.mult, ALU.add))
            then(nc.vector.scalar_tensor_tensor(small[:, 4:5], part[:], float(STEPS), small[:, 3:4],
                                                ALU.mult, ALU.add))
            then(nc.vector.tensor_tensor(small[:, 5:6], small[:, 4:5], small[:, 2:3], ALU.add))
            nc.vector.tensor_copy(fix_row[:], small[:, 5:6])
            then(nc.vector.tensor_scalar(pos_i, cur, 7, None, ALU.arith_shift_right))
            nc.vector.tensor_copy(hi[:], pos_i)
            then(nc.vector.tensor_scalar(pos.bitcast(I32), cur, 127, None, ALU.bitwise_and))
            nc.vector.tensor_copy(lo[:], pos.bitcast(I32))
            then(nc.vector.tensor_scalar(diag[:], ident[:], small[:, 1:2], None, ALU.mult))
            dve.wait_ge(s_bias, 32)
            nc.vector.tensor_tensor(bias[:], bias[:], bias2[:], ALU.add).then_inc(s_const, 1)
            dve.wait_ge(s_const, 1)

            A_PRE = NT - A_LOOP

            def a_out(done, tile):
                dve.wait_ge(s_amm, done + 1)
                nc.vector.tensor_tensor(tile, ps_a[:, 0, :], bias[:], ALU.add).then_inc(s_aev, 1)

            for t in range(A_LOOP, NT):
                a_out(t - A_LOOP, a_sb[:, t, :])
            dve.wait_ge(s_flags, 1)
            then(nc.vector.tensor_scalar(carry_on[:], ps_b[:, 0, 0:P], -2.0, 1.0, ALU.mult, ALU.add))
            nc.vector.tensor_scalar(carry_on[:], carry_on[:], FLT_MAX, None, ALU.mult).then_inc(s_const, 1)

            def fold_turn(turn, gathered, ahead, first, early_at=None, aside={}):
                if not first:
                    dve.wait_ge(s_fold, turn * U)
                nc.vector.tensor_copy(reset_now[:], reset[:, bass.ds(turn * U, U)]).then_inc(s_reset, 1)
                dve.wait_ge(s_reset, turn + 1)
                for g, n in enumerate(GROUPS):
                    if early_at is None:
                        dve.wait_ge(s_got[g], gathered * (16 * n) + 16 * n)
                    if g >= 2:
                        dve.wait_ge(s_copied[g - 2], turn + 1)
                    elif not first:
                        dve.wait_ge(s_copied[g + 2], turn)
                    for s in range(n):
                        k = START[g] + s
                        former = acc[:, ACC0[g] + s - 1, :] if s else hist[:, (k - 1) % U, :]
                        new = acc[:, ACC0[g] + s, :] if s < n - 1 else hist[:, k, :]
                        if early_at is None:
                            row = rows[:, k, :]
                        else:
                            row = early[:, bass.ds(early_at + k, 1), :].rearrange("p a d -> p (a d)")
                        if s == n - 1 and not first:
                            dve.wait_ge(s_hout[g], turn * 16)
                        if not first or k:
                            dve.wait_ge(s_fold, turn * U + k)
                        nc.vector.scalar_tensor_tensor(new, former, reset_now[:, k:k + 1], row,
                                                       ALU.min, ALU.max).then_inc(s_fold, 1)
                    if early_at is None:
                        dve.wait_ge(s_fold, turn * U + (START[g] + n))
                        nc.vector.tensor_copy(stage[:, START[g]:START[g] + n],
                                              idx[:, bass.ds((turn + ahead) * U + START[g], n)]
                                              ).then_inc(s_stage[g], 1)
                    if g in aside:
                        aside[g]()

            def one_hots(share, first):
                if not first:
                    dve.wait_ge(s_hotused, share)
                nc.vector.tensor_tensor(hot_hi[:], cols_b[:, 0:NT].unsqueeze(1).broadcast_to([P, U, NT]),
                                        hi[:, bass.ds(share * U, U)].unsqueeze(2).broadcast_to([P, U, NT]),
                                        ALU.is_equal)
                nc.vector.tensor_tensor(hot_lo[:], cols_b[:].unsqueeze(1).broadcast_to([P, U, P]),
                                        lo[:, bass.ds(share * U, U)].unsqueeze(2).broadcast_to([P, U, P]),
                                        ALU.is_equal).then_inc(s_hot, 1)

            def a_at(t):
                return a_sb[:, bass.ds(t, 1), :].rearrange("p a d -> p (a d)")

            def beside(i, first):
                def tile(j):
                    a_out(i * A_BESIDE + (A_PRE + j), a_at(i * A_BESIDE + j))

                assert A_BESIDE == 2
                fold_turn(i, i, 1, first, aside={0: lambda: tile(0), 1: lambda: one_hots(i, first),
                                                 3: lambda: tile(1)})

            beside(0, True)
            with dve.Fori(1, BESIDE) as i:
                beside(i, False)
            with dve.Fori(0, MIX) as i:
                def tile_and_share(j):
                    a_out(i * A_MIX + (A_PRE + A_BESIDE * BESIDE + j), a_at(i * A_MIX + (A_BESIDE * BESIDE + j)))
                    one_hots(i * MIX_SHARES + (BESIDE + j), False)

                assert A_MIX == MIX_SHARES == MIX_TURNS - 2 and MIX_TURNS == 5
                fold_turn(i * 5 + MIX_AT, i * 4 + BESIDE, 2, False)
                dve.wait_ge(s_cbe, EARLY)
                fold_turn(i * 5 + (MIX_AT + 1), None, None, False, early_at=i * U)
                for q in range(3):
                    fold_turn(i * 5 + (MIX_AT + 2 + q), i * 4 + (BESIDE + 1 + q), 1, False,
                              aside={2: lambda: tile_and_share(q)})
            nc.vector.memset(x_sb[96:P, NT - 1, :], 0.0).then_inc(s_pad, 1)
            with dve.Fori(0, COUNT) as i:
                def share(r):
                    one_hots(i * 2 + (BESIDE + MIX_SHARES * MIX + r), False)

                fold_turn(i + COUNT_AT, i + (BESIDE + (MIX_TURNS - 1) * MIX), 1, False,
                          aside={1: lambda: share(0), 3: lambda: share(1)})

            def sum_counts():
                dve.wait_ge(s_hotused, TURNS + 1)
                nc.vector.tensor_copy(counts[0:NT, :], ps_h[0:NT, 0, 0:P]).then_inc(s_ends, 1)
                nc.vector.tensor_tensor_scan(csum[0:NT, :], ones[0:NT, :], ps_h[0:NT, 0, 0:P], 0.0, ALU.mult,
                                             ALU.add).then_inc(s_csum, 1)

            def find_ends():
                dve.wait_ge(s_csum, 1)
                dve.wait_ge(s_before, 1)
                then(nc.vector.tensor_scalar(small[0:NT, 7:8], ps_a[0:NT, 0, 0:1], -1.0, None, ALU.add))
                nc.vector.tensor_scalar(ends[0:NT, :], csum[0:NT, :], small[0:NT, 7:8], 0.0, ALU.add,
                                        ALU.max).then_inc(s_ends, 1)

            def by_node():
                dve.wait_ge(s_turned, 2)
                nc.vector.tensor_copy(end_row[:], ps_a[:, 0, 0:NT])
                then(nc.vector.tensor_scalar(has[:], ps_h[:, 0, 0:NT], 0.5, 2.0, ALU.is_gt, ALU.mult))
                then(nc.vector.tensor_scalar(has[:], has[:], 1.0, FLT_MAX, ALU.subtract, ALU.mult))

            fold_turn(LAST_AT, GATHERED - LAST, 1, False, aside={1: sum_counts, 2: find_ends, 3: by_node})

            def mask(t):
                nc.vector.tensor_scalar(a_at(t), a_at(t), has[:, bass.ds(t, 1)], None, ALU.min)

            MASKED = NT // (LAST - 1)
            with dve.Fori(0, LAST - 1) as i:
                def masks(these):
                    for j in these:
                        mask(i * MASKED + j)

                fold_turn(i + (LAST_AT + 1), i + (GATHERED - LAST + 1), 1, False,
                          aside={0: lambda: masks(range(0, MASKED // 2)),
                                 2: lambda: masks(range(MASKED // 2, MASKED))})
            for t in range(MASKED * (LAST - 1), NT):
                nc.vector.tensor_scalar(a_sb[:, t, :], a_sb[:, t, :], has[:, t:t + 1], None, ALU.min)
            nc.vector.memset(small[:, 8:9], 0.0).then_inc(s_masked, 1)

            dve.wait_ge(s_lastt, 1)
            for k in range(KC):
                nc.vector.tensor_tensor_scan(scanned[:, k, 1:P + 1], carry_on[:], ps_t[:, 0, k * P:(k + 1) * P],
                                             -FLT_MAX, ALU.min, ALU.max).then_inc(s_scan, 1)
            dve.wait_ge(s_carry, 1)
            dve.wait_ge(s_fixin, 16)
            nc.vector.tensor_tensor(fix[:], fix[:], ps_b[:, 0, :], ALU.max).then_inc(s_fixed, 1)


            def drop_infinite(o, y, ready_sem, ready):
                dve.wait_ge(ready_sem, ready)
                nc.vector.scalar_tensor_tensor(y, y, FLT_MAX, y, ALU.is_le, ALU.mult).then_inc(s_o, 1)

            def statistics(o, y, xs, z, first, tiles, written_sem, written):
                if written_sem is not None:
                    dve.wait_ge(written_sem, written)
                dve.wait_ge(s_o, o)
                nc.vector.scalar_tensor_tensor(z, y, 0.0, xs, ALU.max, ALU.add).then_inc(s_o, 1)
                dve.wait_ge(s_o, o + 1)
                for j in range(tiles):
                    nc.vector.bn_stats(stats[:, first + j, :], z[:, j, :]).then_inc(s_o, 1)
                dve.wait_ge(s_o, o + 1 + tiles)
                dve.nop(nofuse=True)
                for j in range(tiles):
                    last = nc.vector.bn_aggr(meanvar[:, first + j, :], stats[:, first + j, :])
                    last.then_inc(s_o if j < tiles - 1 else s_var, 1)

            def scales(quarters, o, first, tiles):
                these = slice(first, first + tiles)
                dve.wait_ge(s_sd, quarters + 1)
                nc.vector.reciprocal(rstd[:, these], sd[:, these]).then_inc(s_o, 1)
                dve.wait_ge(s_o, o + 1)
                nc.vector.scalar_tensor_tensor(shift[:, these], meanvar[:, these, 0], -1.0, rstd[:, these],
                                               ALU.mult, ALU.mult).then_inc(s_scale, 1)

            PER_QUARTER = 2 + 2 * QUARTER
            dve.wait_ge(s_x, 16 * (X_LOADS + 1))
            for g in range(NG):
                dve.wait_ge(s_hout[g], 16 * TURNS)

            def out_turn(c, first):
                for q in range(4):
                    o = c * (4 * PER_QUARTER) + (q * PER_QUARTER - (q > 0))
                    tiles = bass.ds(c * 4 * QUARTER + q * QUARTER, QUARTER)
                    z = hist[:, q * QUARTER:(q + 1) * QUARTER, :]
                    drop_infinite(o, a_sb[:, tiles, :], s_end[q], (c + 1) * (16 * QUARTER))
                    if q:
                        scales(c * 4 + (q - 1), o + 1, (q - 1) * QUARTER, QUARTER)
                    statistics(o + (2 if q else 1), a_sb[:, tiles, :], x_sb[:, tiles, :], z, q * QUARTER, QUARTER,
                               None if first else s_out[q], c * 16)
                scales(c * 4 + 3, c * (4 * PER_QUARTER) + (4 * PER_QUARTER - 1), 3 * QUARTER, QUARTER)

            out_turn(0, True)
            with dve.Fori(1, OUT_TURNS) as c:
                out_turn(c, False)
            o = OUT_TURNS * 4 * PER_QUARTER
            drop_infinite(o, a_sb[:, NT - 1:NT, :], s_end[0], 16 * (QUARTER * OUT_TURNS + 1))
            statistics(o + 1, a_sb[:, NT - 1:NT, :], x_sb[:, NT - 1:NT, :], hist[:, U - 1:U, :], 0, 1, None, 0)
            scales(4 * OUT_TURNS, o + 3, 0, 1)


_INS = ["x", "xt", "src", "dst", "theta_t", "phi_t", "theta_b", "phi_b"]


def kernel(x, src, dst, L0_gnn_theta_w, L0_gnn_theta_b, L0_gnn_phi_w, L0_gnn_phi_b):
    import numpy as np
    import concourse.bacc as bacc
    from concourse.bass_utils import run_bass_kernel_spmd

    x = np.asarray(x)
    n, d = x.shape
    tiles = (n + P - 1) // P
    padded = np.zeros((tiles * P, d), x.dtype)
    padded[:n] = x
    xt = padded.reshape(tiles, P, d // P, P).transpose(0, 3, 2, 1)
    arrays = {
        "x": x, "xt": xt, "src": np.asarray(src), "dst": np.asarray(dst),
        "theta_t": np.asarray(L0_gnn_theta_w).T, "phi_t": np.asarray(L0_gnn_phi_w).T,
        "theta_b": np.asarray(L0_gnn_theta_b), "phi_b": np.asarray(L0_gnn_phi_b),
    }
    nc = bacc.Bacc("TRN2", target_bir_lowering=False, num_devices=1)
    ins, args = {}, []
    for name in _INS:
        a = np.ascontiguousarray(arrays[name])
        ins[f"in_{name}"] = a
        args.append(nc.dram_tensor(f"in_{name}", a.shape, mybir.dt.from_np(a.dtype), kind="ExternalInput").ap())
    out = nc.dram_tensor("out", (n, d), F32, kind="ExternalOutput").ap()
    build(nc, *args, out)
    r = run_bass_kernel_spmd(nc, [ins], core_ids=[0])
    return r.results[0]["out"]
```

```python
from contextlib import ExitStack

import concourse.bass as bass
from concourse import mybir

P = 128
ALU = mybir.AluOpType
ACT = mybir.ActivationFunctionType
F32 = mybir.dt.float32
BF16 = mybir.dt.bfloat16
I32 = mybir.dt.int32
AX_X = mybir.AxisListType.X
FLT_MAX = 3.4028234663852886e38
EPS = 1e-5

CHUNK = 7
PARTS = (4, 3)
GROUPS = (5, 4, 4, 4)
QUARTER = 4


def build(nc, x, xt, src, dst, theta_t, phi_t, theta_b, phi_b, out):
    N, D = x.shape
    E = src.shape[0]
    NT = (N + P - 1) // P
    KC = D // P
    STEPS = (E + P - 1) // P
    U = sum(GROUPS)
    NG = len(GROUPS)
    START = [sum(GROUPS[:g]) for g in range(NG)]
    TURNS = STEPS // U
    FULL_P = E // STEPS
    REST = E - FULL_P * STEPS
    MIX = 3
    MIX_TURNS = 5
    EARLY = MIX * U
    CONVERT = 3
    BESIDE = EARLY // CONVERT
    MIX_SHARES = 3
    COUNT = (TURNS - BESIDE - MIX_SHARES * MIX) // 2
    LAST = TURNS - BESIDE - MIX_TURNS * MIX - COUNT
    MIX_AT, COUNT_AT = BESIDE, BESIDE + MIX_TURNS * MIX
    LAST_AT = COUNT_AT + COUNT
    GATHERED = TURNS - MIX
    A_BESIDE, A_MIX = 2, 3
    A_LOOP = A_BESIDE * BESIDE + A_MIX * MIX
    CHUNKS = NT // CHUNK
    assert GROUPS[0] <= CHUNK and GROUPS[1] <= CHUNK - A_MIX and max(GROUPS[2:]) <= GROUPS[1]
    assert STEPS % U == 0 and NT % CHUNK == 0 and CHUNKS % 2 == 1 and D % P == 0 and FULL_P == P - 1
    assert BESIDE + MIX_SHARES * MIX + 2 * COUNT == TURNS and LAST > 1 and sum(PARTS) == CHUNK and NT - CHUNK <= A_LOOP <= NT
    X_TILES = 4
    X_LOADS = (NT - 1) // X_TILES
    assert X_LOADS * X_TILES == NT - 1 and X_LOADS < COUNT + LAST
    ACC0 = (0, 4, 0, 4)
    OUT_TURNS = (NT - 1) // (4 * QUARTER)
    assert OUT_TURNS * 4 * QUARTER == NT - 1 and U == 4 * QUARTER + 1
    LAST_ROWS = N - (NT - 1) * P
    FAR = 1 << 20

    with ExitStack() as ctx:
        def sb(name, shape, dt=F32):
            return ctx.enter_context(nc.sbuf_tensor(name, shape, dt))

        def ps(name, shape):
            return ctx.enter_context(nc.psum_tensor(name, shape, F32))

        def sem(name):
            return ctx.enter_context(nc.semaphore(name))

        b_table = nc.dram_tensor("b_table", (NT * P, D), F32).ap()
        runmax = nc.dram_tensor("runmax", (P * STEPS, D), F32).ap()
        runmax_by_p = runmax.rearrange("(p k) d -> p k d", p=P)

        xt_sb = sb("xt_sb", [P, 2 * CHUNK, KC, P])
        converted_rows = xt_sb[:].rearrange("p j k n -> p j (k n)")
        CONVERTED0 = (0, CHUNK + A_MIX)
        theta_sb = sb("theta_sb", [P, KC, D])
        diff_sb = sb("diff_sb", [P, KC, D])
        bias = sb("bias", [P, D])
        bias2 = sb("bias2", [P, D])
        early = sb("early", [P, max(EARLY, NT), D])
        x_sb = early[:, 0:NT, :]
        a_sb = sb("a_sb", [P, NT, D])
        rows = sb("rows", [P, U, D])
        hist = sb("hist", [P, U, D])
        idx = sb("idx", [P, STEPS + 2 * U], I32)
        stage = sb("stage", [P, U], I32)
        reset = sb("reset", [P, STEPS])
        reset_now = sb("reset_now", [P, U])
        hi = sb("hi", [P, STEPS], BF16)
        lo = sb("lo", [P, STEPS], BF16)
        hot_hi = sb("hot_hi", [P, U, NT], BF16)
        hot_lo = sb("hot_lo", [P, U, P], BF16)
        conv_in = sb("conv_in", [P, CONVERT, D])
        conv_t = sb("conv_t", [P, KC, P])
        cols_i = sb("cols_i", [P, P], I32)
        part_i = sb("part_i", [P, 1], I32)
        cols = sb("cols", [P, P])
        cols_b = sb("cols_b", [P, P], BF16)
        part = sb("part", [P, 1])
        ident = sb("ident", [P, P])
        ones = sb("ones", [P, P])
        below = sb("below", [P, NT])
        zero_b = sb("zero_b", [P, P], BF16)
        small = sb("small", [P, 16])
        fix_row = sb("fix_row", [P, 1], I32)
        diag = sb("diag", [P, P])
        carry_on = sb("carry_on", [P, P])
        scanned = sb("scanned", [P, KC, P + 1])
        fix = sb("fix", [P, D])
        counts = sb("counts", [P, P])
        csum = sb("csum", [P, P])
        ends = sb("ends", [P, P])
        end_row = sb("end_row", [P, NT], I32)
        has = sb("has", [P, NT])
        stats = sb("stats", [P, 4 * QUARTER + 1, 6])
        meanvar = sb("meanvar", [P, 4 * QUARTER + 1, 2])
        sd = sb("sd", [P, 4 * QUARTER + 1])
        eps = sb("eps", [P, 1])
        rstd = sb("rstd", [P, 4 * QUARTER + 1])
        shift = sb("shift", [P, 4 * QUARTER + 1])
        hist_flat = hist[:].rearrange("p u d -> p (u d)")
        dwin = hist_flat[:, 0:STEPS + 2].bitcast(I32)
        flag = hist_flat[:, 1000:1000 + STEPS]
        pos = hist_flat[:, 2000:2000 + STEPS]
        pos_i = hist_flat[:, 3000:3000 + STEPS].bitcast(I32)
        assert STEPS + 2 <= 1000 and (U - 1) * D >= 3000 + STEPS

        acc = ps("acc", [P, 8, D])
        ps_t = ps("ps_t", [P, 2, D])
        ps_b = ps("ps_b", [P, 2, D])
        ps_a = ps("ps_a", [P, 2, D])
        ps_h = ps("ps_h", [P, 2, D])
        b_psum = [acc[:, 0, :], acc[:, 2, :], acc[:, 4, :], acc[:, 6, :], ps_t[:, 0, :], ps_b[:, 0, :],
                  ps_a[:, 0, :]]
        assert len(b_psum) == CHUNK

        s_w = sem("weights_loaded")
        s_xt = [[sem(f"xt_chunk_loaded{h}_{part}") for part in range(2)] for h in range(2)]
        s_at = [sem(f"xt_tile_loaded{j}") for j in range(A_MIX)]
        s_idx = sem("src_loaded")
        s_dst = sem("dst_loaded")
        s_bias = sem("bias_loaded")
        s_x = sem("x_loaded")
        s_iota = sem("iotas_made")
        s_diff = sem("diff_made")
        s_bmm = sem("b_tile_in_psum")
        s_bev = sem("b_tile_evacuated")
        s_bout = [sem(f"b_chunk_written{h}") for h in range(2)]
        s_prep = sem("prep_steps")
        s_pad = sem("pads_cleared")
        s_const = sem("constants_ready")
        s_flags = sem("flags_spread")
        s_xrows = sem("x_rows_gathered")
        s_cin = sem("conversion_staged")
        s_ct = sem("rows_transposed")
        s_cte = sem("transposed_rows_copied")
        s_cb = sem("rows_converted")
        s_cbe = sem("converted_rows_copied")
        s_now = sem("converted_rows_staged")
        s_amm = sem("a_tile_in_psum")
        s_aev = sem("a_tile_evacuated")
        s_stage = [sem(f"indices_staged{g}") for g in range(NG)]
        s_got = [sem(f"rows_gathered{g}") for g in range(NG)]
        s_got_end = sem("turns_last_row_gathered")
        s_reset = sem("resets_staged")
        s_fold = sem("steps_folded")
        s_copied = [sem(f"maxima_copied{g}") for g in range(NG)]
        s_hout = [sem(f"maxima_written{g}") for g in range(NG)]
        s_hot = sem("one_hots_made")
        s_hotused = sem("one_hots_used")
        s_csum = sem("counts_summed")
        s_before = sem("edges_before_tiles")
        s_ends = sem("last_edges_by_tile")
        s_turned = sem("last_edges_and_counts_turned")
        s_masked = sem("empty_nodes_masked")
        s_lastt = sem("last_maxima_transposed")
        s_scan = sem("partitions_scanned")
        s_carry = sem("carries_by_partition")
        s_fixin = sem("fix_rows_gathered")
        s_fixed = sem("fix_rows_ready")
        s_fixout = sem("fix_rows_written")
        s_end_short = sem("end_rows_added_short")
        s_end = [sem(f"end_rows_added{q}") for q in range(4)]
        s_o = sem("output_steps")
        s_var = sem("variances_ready")
        s_sd = sem("deviations_ready")
        s_scale = sem("scales_ready")
        s_norm = sem("tiles_normalised")
        s_out_short = sem("output_written_short")
        s_out = [sem(f"output_written{q}") for q in range(4)]

        def a_tile(j):
            return CHUNK + j

        block = ctx.enter_context(nc.Block())

        @block.sync
        def _(sp):
            by_chunk = xt.rearrange("(c j) p k n -> c p j (k n)", j=CHUNK)
            xt_flat = xt_sb[:].rearrange("p j k n -> p j (k n)")
            table = b_table.rearrange("(c j p) d -> c p j d", j=CHUNK, p=P)

            def tiles_of(part):
                return slice(PARTS[0] * part, PARTS[0] + PARTS[1] * part)

            def load(c, h, part):
                at = tiles_of(part)
                sp.dma_start(xt_flat[:, h * CHUNK + at.start:h * CHUNK + at.stop],
                             by_chunk[c][:, at]).then_inc(s_xt[h][part], 16)

            def load_at(c, h, part):
                at = tiles_of(part)
                sp.dma_start(xt_flat[:, h * CHUNK + at.start:h * CHUNK + at.stop],
                             by_chunk[bass.ds(c, 1), :, at].rearrange("a p j n -> p (a j) n")
                             ).then_inc(s_xt[h][part], 16)

            def store_at(c, h):
                sp.dma_start(table[bass.ds(c, 1)].rearrange("a p j d -> p (a j) d"),
                             rows[:, h * CHUNK:(h + 1) * CHUNK, :]).then_inc(s_bout[h], 16)

            sp.dma_start(theta_sb[:], theta_t.rearrange("(c p) d -> p c d", p=P)).then_inc(s_w, 16)
            sp.dma_start(diff_sb[:], phi_t.rearrange("(c p) d -> p c d", p=P)).then_inc(s_w, 16)
            sp.wait_ge(s_pad, 1)
            sp.dma_start(idx[0:FULL_P, 0:STEPS],
                         src[0:FULL_P * STEPS].rearrange("(p k) -> p k", k=STEPS)).then_inc(s_idx, 16)
            sp.dma_start(idx[FULL_P:P, 0:REST],
                         src[FULL_P * STEPS:E].rearrange("(p k) -> p k", p=1)).then_inc(s_idx, 16)
            for c in range(2):
                for part in range(2):
                    load(c, c, part)
            sp.wait_ge(s_bmm, PARTS[0])
            load(2, 0, 0)
            sp.wait_ge(s_bmm, CHUNK)
            load(2, 0, 1)
            sp.wait_ge(s_bev, CHUNK)
            sp.dma_start(table[0], rows[:, 0:CHUNK, :]).then_inc(s_bout[0], 16)
            with sp.Fori(1, (CHUNKS - 1) // 2) as m:
                for h in (1, 0):
                    before = m * 2 * CHUNK - CHUNK * h
                    sp.wait_ge(s_bmm, before + PARTS[0])
                    load_at(m * 2 + (2 - h), h, 0)
                    sp.wait_ge(s_bmm, before + CHUNK)
                    load_at(m * 2 + (2 - h), h, 1)
                    sp.wait_ge(s_bev, before + CHUNK)
                    store_at(m * 2 - h, h)
            sp.wait_ge(s_bev, (CHUNKS - 1) * CHUNK)
            sp.dma_start(table[CHUNKS - 2], rows[:, CHUNK:2 * CHUNK, :]).then_inc(s_bout[1], 16)
            sp.wait_ge(s_bev, NT)
            sp.dma_start(table[CHUNKS - 1], rows[:, 0:CHUNK, :]).then_inc(s_bout[0], 16)
            sp.wait_ge(s_bmm, (CHUNKS - 1) * CHUNK)
            for j in range(A_MIX):
                t = j if j < A_BESIDE else A_BESIDE * BESIDE + j
                sp.dma_start(xt_flat[:, a_tile(j)], xt[t].rearrange("p k n -> p (k n)")).then_inc(s_at[j], 16)

            def maxima_out(turn):
                for g, n in enumerate(GROUPS):
                    sp.wait_ge(s_copied[g], turn + 1)
                    sp.dma_start(runmax_by_p[:, bass.ds(turn * U + START[g], n), :],
                                 hist[:, START[g]:START[g] + n, :]).then_inc(s_hout[g], 16)

            def next_tiles(done, first, n):
                sp.wait_ge(s_amm, done)
                for j in range(n):
                    sp.dma_start(xt_flat[:, a_tile(j):a_tile(j) + 1],
                                 xt[bass.ds(first + j, 1)].rearrange("a p k n -> p a (k n)")
                                 ).then_inc(s_at[j], 16)

            A_PRE = NT - A_LOOP
            with sp.Fori(0, BESIDE) as i:
                maxima_out(i)
                next_tiles(i * A_BESIDE + (A_PRE + A_BESIDE), i * A_BESIDE + A_BESIDE, A_BESIDE)
            with sp.Fori(0, MIX) as i:
                for q in range(MIX_TURNS):
                    maxima_out(i * MIX_TURNS + (MIX_AT + q))
                next_tiles(i * A_MIX + (A_PRE + A_BESIDE * BESIDE + A_MIX),
                           i * A_MIX + (A_BESIDE * BESIDE + A_MIX), A_MIX)
            sp.wait_ge(s_fold, COUNT_AT * U)
            sp.wait_ge(s_pad, 3)
            sp.dma_start(x_sb[0:LAST_ROWS, NT - 1, :], x[(NT - 1) * P:N]).then_inc(s_x, 16)
            by_load = x[0:(NT - 1) * P].rearrange("(c t p) d -> c p t d", p=P, t=X_TILES)
            with sp.Fori(0, X_LOADS) as i:
                maxima_out(i + COUNT_AT)
                sp.dma_start(x_sb[:, bass.ds(i * X_TILES, X_TILES), :],
                             by_load[bass.ds(i, 1)].rearrange("a p t d -> p (a t) d")).then_inc(s_x, 16)
            with sp.Fori(COUNT_AT + X_LOADS, TURNS) as turn:
                maxima_out(turn)

            sp.wait_ge(s_norm, 1)
            sp.dma_start(out[(NT - 1) * P:N], hist[0:LAST_ROWS, U - 1, :]).then_inc(s_out_short, 16)
            out_tiles = out[0:(NT - 1) * P].rearrange("(t p) d -> p t d", p=P)
            with sp.Fori(0, OUT_TURNS) as c:
                for q in range(4):
                    sp.wait_ge(s_norm, c * 4 * QUARTER + ((q + 1) * QUARTER + 1))
                    sp.dma_start(out_tiles[:, bass.ds(c * 4 * QUARTER + q * QUARTER, QUARTER), :],
                                 hist[:, q * QUARTER:(q + 1) * QUARTER, :]).then_inc(s_out[q], 16)
            sp.wait_ge(s_out_short, 16)
            for q in range(4):
                sp.wait_ge(s_out[q], 16 * OUT_TURNS)

        @block.gpsimd
        def _(pool):
            nc.gpsimd.iota(cols_i[:], pattern=[[1, P]], base=0, channel_multiplier=0).then_inc(s_iota, 1)
            nc.gpsimd.iota(part_i[:], pattern=[[1, 1]], base=0, channel_multiplier=1).then_inc(s_iota, 1)
            nc.gpsimd.iota(pos_i, pattern=[[1, STEPS]], base=0, channel_multiplier=0).then_inc(s_iota, 1)
            pool.wait_ge(s_idx, 32)
            for m in range(MIX):
                for s in range(U):
                    k = (MIX_AT + MIX_TURNS * m + 1) * U + s
                    pool.indirect_dma_start(
                        out=early[:, m * U + s, :], out_offset=None, in_=x,
                        in_offset=bass.IndirectOffsetOnAxis(ap=idx[:, k:k + 1], axis=0)
                    ).then_inc(s_xrows, 16)
            pool.wait_ge(s_bout[0], 16 * (CHUNKS + 1) // 2)
            pool.wait_ge(s_bout[1], 16 * (CHUNKS // 2))
            with pool.Fori(0, GATHERED) as i:
                for g, n in enumerate(GROUPS):
                    pool.wait_ge(s_stage[g], i + 1)
                    pool.nop(nofuse=True)
                    for s in range(START[g], START[g] + n):
                        pool.indirect_dma_start(
                            out=rows[:, s, :], out_offset=None, in_=b_table,
                            in_offset=bass.IndirectOffsetOnAxis(ap=stage[:, s:s + 1], axis=0)
                        ).then_inc(s_got[g] if s < U - 1 else s_got_end, 16)
            for g in range(NG):
                pool.wait_ge(s_hout[g], 16 * TURNS)
            pool.wait_ge(s_masked, 1)
            pool.indirect_dma_start(
                out=fix[:], out_offset=None, in_=runmax,
                in_offset=bass.IndirectOffsetOnAxis(ap=fix_row[:], axis=0),
                bounds_check=E - 1, oob_is_err=False).then_inc(s_fixin, 16)
            pool.wait_ge(s_fixed, 1)
            pool.indirect_dma_start(
                out=runmax, out_offset=bass.IndirectOffsetOnAxis(ap=fix_row[:], axis=0), in_=fix[:],
                in_offset=None, bounds_check=E - 1, oob_is_err=False).then_inc(s_fixout, 16)
            pool.wait_ge(s_fixout, 16)
            def add_maxima(t, ready):
                pool.indirect_dma_start(
                    out=a_sb[:, t, :], out_offset=None, in_=runmax,
                    in_offset=bass.IndirectOffsetOnAxis(ap=end_row[:, t:t + 1], axis=0),
                    compute_op=ALU.add).then_inc(ready, 16)

            add_maxima(NT - 1, s_end_short)
            for t in range(NT - 1):
                turn, q = divmod(t // QUARTER, 4)
                if turn and t % QUARTER == 0:
                    pool.wait_ge(s_end[q], 16 * QUARTER * turn)
                add_maxima(t, s_end[q])

        @block.scalar
        def _(act):
            act.wait_ge(s_pad, 2)
            act.wait_ge(s_w, 32)
            act.dma_start(dwin[0:FULL_P, 1:STEPS + 1],
                          dst[0:FULL_P * STEPS].rearrange("(p k) -> p k", k=STEPS)).then_inc(s_dst, 16)
            act.dma_start(dwin[FULL_P:P, 1:REST + 1],
                          dst[FULL_P * STEPS:E].rearrange("(p k) -> p k", p=1)).then_inc(s_dst, 16)
            ends_of_runs = dst[0:FULL_P * STEPS].rearrange("(p k) -> p k", k=STEPS)
            with nc.allow_non_contiguous_dma(reason="one number per partition"):
                act.dma_start(dwin[1:P, 0:1], ends_of_runs[:, STEPS - 1:STEPS]).then_inc(s_dst, 16)
                starts = dst[STEPS:FULL_P * STEPS].rearrange("(p k) -> p k", k=STEPS)
                act.dma_start(dwin[0:FULL_P - 1, STEPS + 1:STEPS + 2], starts[:, 0:1]).then_inc(s_dst, 16)
                act.dma_start(dwin[FULL_P - 1:FULL_P, STEPS + 1:STEPS + 2],
                              dst[FULL_P * STEPS:FULL_P * STEPS + 1].rearrange("(p k) -> p k", p=1)
                              ).then_inc(s_dst, 16)
            act.dma_start(bias[:], theta_b.rearrange("(a d) -> a d", a=1).broadcast_to([P, D])).then_inc(s_bias, 16)
            act.dma_start(bias2[:], phi_b.rearrange("(a d) -> a d", a=1).broadcast_to([P, D])).then_inc(s_bias, 16)

            def evacuate(base, h):
                for j in range(CHUNK):
                    act.wait_ge(s_bmm, base + j + 1)
                    nc.scalar.copy(rows[:, h * CHUNK + j, :], b_psum[j]).then_inc(s_bev, 1)

            evacuate(0, 0)
            evacuate(CHUNK, 1)
            act.wait_ge(s_bout[0], 16)
            evacuate(2 * CHUNK, 0)
            with act.Fori(2, (CHUNKS - 1) // 2 + 1) as m:
                for h in (1, 0):
                    act.wait_ge(s_bout[h], m * 16 - 16 * h)
                    evacuate(m * 2 * CHUNK - h * CHUNK, h)
            act.wait_ge(s_const, 1)

            def maxima_copy(turn, g, first):
                act.wait_ge(s_fold, turn * U + (START[g] + GROUPS[g]))
                if not first:
                    act.wait_ge(s_hout[g], turn * 16)
                nc.scalar.copy(hist[:, START[g]:START[g] + GROUPS[g] - 1, :],
                               acc[:, ACC0[g]:ACC0[g] + GROUPS[g] - 1, :]).then_inc(s_copied[g], 1)

            def transposed(i, r):
                act.wait_ge(s_ct, i * CONVERT + (r + 1))
                nc.scalar.copy(conv_t[:].rearrange("p k n -> p (k n)"), ps_t[:, 0, :]).then_inc(s_cte, 1)

            def converted(i, r):
                act.wait_ge(s_cb, i * CONVERT + (r + 1))
                act.nop(nofuse=True)
                nc.scalar.copy(early[:, bass.ds(i * CONVERT + r, 1), :].rearrange("p a d -> p (a d)"),
                               ps_b[:, 0, :]).then_inc(s_cbe, 1)

            def beside(i, first):
                if first:
                    act.wait_ge(s_xrows, 16 * EARLY)
                else:
                    act.wait_ge(s_ct, i * CONVERT)
                    act.nop(nofuse=True)
                nc.scalar.copy(conv_in[:], early[:, bass.ds(i * CONVERT, CONVERT), :]).then_inc(s_cin, 1)
                for g in range(NG):
                    maxima_copy(i, g, first)
                    if g > 0:
                        converted(i, g - 1)
                    if g < CONVERT:
                        transposed(i, g)

            assert NG == CONVERT + 1
            beside(0, True)
            with act.Fori(1, BESIDE) as i:
                beside(i, False)

            def stage_converted(i, g):
                nc.scalar.copy(converted_rows[:, CONVERTED0[g % 2]:CONVERTED0[g % 2] + GROUPS[g], :],
                               early[:, bass.ds(i * U + START[g], GROUPS[g]), :]).then_inc(s_now, 1)

            act.wait_ge(s_cbe, EARLY)
            with act.Fori(0, MIX) as i:
                for g in range(2):
                    stage_converted(i, g)
                for g in range(NG):
                    maxima_copy(i * MIX_TURNS + MIX_AT, g, False)
                for g in range(NG):
                    if g + 2 < NG:
                        act.wait_ge(s_fold, i * (MIX_TURNS * U) + ((MIX_AT + 1) * U + START[g] + GROUPS[g]))
                        act.nop(nofuse=True)
                        stage_converted(i, g + 2)
                    maxima_copy(i * MIX_TURNS + (MIX_AT + 1), g, False)
                for q in range(2, MIX_TURNS):
                    for g in range(NG):
                        maxima_copy(i * MIX_TURNS + (MIX_AT + q), g, False)
            with act.Fori(COUNT_AT, TURNS) as turn:
                for g in range(NG):
                    maxima_copy(turn, g, False)
            for g in range(NG):
                act.wait_ge(s_hout[g], 16 * TURNS)

            def deviation(before, first, tiles):
                act.wait_ge(s_var, before + 1)
                these = slice(first, first + tiles)
                nc.scalar.activation(sd[:, these], meanvar[:, these, 1], ACT.Sqrt,
                                     bias=eps[:, 0:1]).then_inc(s_sd, 1)

            def normalise(before, first, tiles):
                act.wait_ge(s_scale, before + 1)
                for j in range(first, first + tiles):
                    nc.scalar.activation(hist[:, j, :], hist[:, j, :], ACT.Identity, scale=rstd[:, j:j + 1],
                                         bias=shift[:, j:j + 1]).then_inc(s_norm, 1)

            deviation(0, U - 1, 1)
            normalise(0, U - 1, 1)
            with act.Fori(0, OUT_TURNS) as c:
                for q in range(4):
                    deviation(c * 4 + (q + 1), q * QUARTER, QUARTER)
                    normalise(c * 4 + (q + 1), q * QUARTER, QUARTER)

        @block.tensor
        def _(pe):
            def table(base, h, loaded, first):
                for j in range(CHUNK):
                    if j in (0, PARTS[0]):
                        pe.wait_ge(s_xt[h][j > 0], loaded)
                    if not first:
                        pe.wait_ge(s_bev, base - CHUNK + j + 1)
                    for k in range(KC):
                        mm = pe.matmul(b_psum[j], xt_sb[:, h * CHUNK + j, k, :], diff_sb[:, k, :],
                                       start=(k == 0), stop=(k == KC - 1))
                    mm.then_inc(s_bmm, 1)

            pe.wait_ge(s_diff, 1)
            table(0, 0, 16, True)
            with pe.Fori(1, (CHUNKS - 1) // 2 + 1) as m:
                for h in (1, 0):
                    table(m * 2 * CHUNK - h * CHUNK, h, m * 16 + 16 * (1 - h), False)

            A_PRE = NT - A_LOOP

            def a_product(done, slot):
                pe.wait_ge(s_aev, done)
                for k in range(KC):
                    mm = pe.matmul(ps_a[:, 0, :], xt_sb[:, slot, k, :], theta_sb[:, k, :],
                                   start=(k == 0), stop=(k == KC - 1))
                mm.then_inc(s_amm, 1)

            pe.wait_ge(s_bev, NT)
            for t in range(A_LOOP, NT):
                k0 = t - A_LOOP
                if k0:
                    a_product(k0, t % CHUNK)
                else:
                    for k in range(KC):
                        mm = pe.matmul(ps_a[:, 0, :], xt_sb[:, t % CHUNK, k, :], theta_sb[:, k, :],
                                       start=(k == 0), stop=(k == KC - 1))
                    mm.then_inc(s_amm, 1)
            pe.wait_ge(s_const, 1)
            pe.matmul(ps_b[:, 0, 0:P], ones[:], diag[:], start=True, stop=True).then_inc(s_flags, 1)
            pe.matmul(ps_h[0:NT, 0, 0:P], zero_b[:, 0:NT], zero_b[:], start=True, stop=False,
                      skip_group_check=True)
            pe.wait_ge(s_const, 2)

            def count(share):
                pe.wait_ge(s_hot, share + 1)
                for s in range(U):
                    mm = pe.matmul(ps_h[0:NT, 0, 0:P], hot_hi[:, s, :], hot_lo[:, s, :],
                                   start=False, stop=False, skip_group_check=True)
                mm.then_inc(s_hotused, 1)

            def convert(i, r, first):
                if not first or r:
                    pe.wait_ge(s_cte, i * CONVERT + r)
                for k in range(KC):
                    mm = pe.transpose(ps_t[:, 0, k * P:(k + 1) * P], conv_in[:, r, k * P:(k + 1) * P], ident[:])
                mm.then_inc(s_ct, 1)
                if not first or r:
                    pe.wait_ge(s_cbe, i * CONVERT + r)
                pe.wait_ge(s_cte, i * CONVERT + (r + 1))
                for k in range(KC):
                    mm = pe.matmul(ps_b[:, 0, :], conv_t[:, k, :], diff_sb[:, k, :],
                                   start=(k == 0), stop=(k == KC - 1))
                mm.then_inc(s_cb, 1)

            def beside(i, first):
                for j in range(A_BESIDE):
                    pe.wait_ge(s_at[j], i * 16 + 16)
                    a_product(i * A_BESIDE + (A_PRE + j), a_tile(j))
                    if j == 0:
                        pe.wait_ge(s_cin, i + 1)
                        for r in range(CONVERT):
                            convert(i, r, first)
                count(i)

            beside(0, True)
            with pe.Fori(1, BESIDE) as i:
                beside(i, False)
            with pe.Fori(0, MIX) as i:
                for j in range(A_MIX):
                    pe.wait_ge(s_at[j], i * 16 + (16 + 16 * BESIDE * (j < A_BESIDE)))
                    a_product(i * A_MIX + (A_PRE + A_BESIDE * BESIDE + j), a_tile(j))
                    count(i * MIX_SHARES + (BESIDE + j))
            with pe.Fori(BESIDE + MIX_SHARES * MIX, TURNS) as share:
                count(share)
            pe.matmul(ps_h[0:NT, 0, 0:P], zero_b[:, 0:NT], zero_b[:], start=False, stop=True,
                      skip_group_check=True).then_inc(s_hotused, 1)
            pe.wait_ge(s_aev, NT)
            pe.wait_ge(s_csum, 1)
            pe.matmul(ps_a[0:NT, 0, 0:1], below[0:NT, :], csum[0:NT, P - 1:P], start=True,
                      stop=True).then_inc(s_before, 1)
            pe.wait_ge(s_ends, 2)
            pe.transpose(ps_a[:, 0, 0:NT], ends[0:NT, :], ident[0:NT, 0:NT]).then_inc(s_turned, 1)
            pe.transpose(ps_h[:, 0, 0:NT], counts[0:NT, :], ident[0:NT, 0:NT]).then_inc(s_turned, 1)
            pe.wait_ge(s_cbe, EARLY)
            pe.wait_ge(s_fold, STEPS)
            for k in range(KC):
                mm = pe.transpose(ps_t[:, 0, k * P:(k + 1) * P], hist[:, U - 1, k * P:(k + 1) * P], ident[:])
            mm.then_inc(s_lastt, 1)
            pe.wait_ge(s_scan, KC)
            for k in range(KC):
                mm = pe.transpose(ps_b[:, 0, k * P:(k + 1) * P], scanned[:, k, 0:P], ident[:])
            mm.then_inc(s_carry, 1)

        @block.vector
        def _(dve):
            prep = [0]

            def then(ins):
                prep[0] += 1
                ins.then_inc(s_prep, 1)
                dve.wait_ge(s_prep, prep[0])

            nc.vector.memset(idx[96:P, REST:STEPS], 0)
            nc.vector.memset(idx[:, STEPS:], 0).then_inc(s_pad, 1)
            nc.vector.memset(dwin[96:P, REST:STEPS + 1], -1)
            nc.vector.memset(dwin[:, 0:1], -1)
            nc.vector.memset(dwin[:, STEPS + 1:STEPS + 2], -1).then_inc(s_pad, 1)
            dve.wait_ge(s_w, 32)
            nc.vector.tensor_tensor(diff_sb[:], diff_sb[:], theta_sb[:], ALU.subtract).then_inc(s_diff, 1)
            dve.wait_ge(s_idx, 32)
            for g, n in enumerate(GROUPS):
                nc.vector.tensor_copy(stage[:, START[g]:START[g] + n],
                                      idx[:, START[g]:START[g] + n]).then_inc(s_stage[g], 1)
            dve.wait_ge(s_iota, 3)
            nc.vector.tensor_copy(cols[:], cols_i[:])
            nc.vector.tensor_copy(cols_b[:], cols_i[:])
            nc.vector.tensor_copy(pos, pos_i)
            then(nc.vector.tensor_copy(part[:], part_i[:]))
            nc.vector.tensor_scalar(ident[:], cols[:], part[:, 0:1], None, ALU.is_equal)
            nc.vector.tensor_scalar(below[:], cols[:, 0:NT], part[:, 0:1], None, ALU.is_gt)
            nc.vector.memset(ones[:], 1.0)
            nc.vector.memset(zero_b[:], 0.0)
            nc.vector.memset(fix[:], 0.0)
            nc.vector.memset(eps[:], EPS)
            nc.vector.memset(scanned[:, :, 0:1], 0.0)
            nc.vector.memset(hist[:, U - 1, :], -FLT_MAX)
            dve.wait_ge(s_dst, 80)
            cur, before, after = dwin[:, 1:STEPS + 1], dwin[:, 0:STEPS], dwin[:, 2:STEPS + 2]
            then(nc.vector.tensor_tensor(flag, cur, before, ALU.not_equal))
            nc.vector.tensor_copy(small[:, 0:1], flag[:, 0:1])
            nc.vector.tensor_scalar(reset[:], flag, -2.0, 1.0, ALU.mult, ALU.add)
            then(nc.vector.tensor_reduce(small[:, 1:2], flag, AX_X, ALU.max))
            nc.vector.tensor_scalar(reset[:], reset[:], FLT_MAX, None, ALU.mult)
            then(nc.vector.tensor_tensor(flag, cur, after, ALU.not_equal))
            then(nc.vector.scalar_tensor_tensor(flag, flag, -4096.0, pos, ALU.mult, ALU.add))
            then(nc.vector.tensor_reduce(small[:, 2:3], flag, AX_X, ALU.min))
            then(nc.vector.scalar_tensor_tensor(small[:, 3:4], small[:, 2:3], 0.0, small[:, 0:1],
                                                ALU.is_ge, ALU.add))
            then(nc.vector.tensor_scalar(small[:, 3:4], small[:, 3:4], float(FAR), 4096.0, ALU.mult, ALU.add))
            then(nc.vector.scalar_tensor_tensor(small[:, 4:5], part[:], float(STEPS), small[:, 3:4],
                                                ALU.mult, ALU.add))
            then(nc.vector.tensor_tensor(small[:, 5:6], small[:, 4:5], small[:, 2:3], ALU.add))
            nc.vector.tensor_copy(fix_row[:], small[:, 5:6])
            then(nc.vector.tensor_scalar(pos_i, cur, 7, None, ALU.arith_shift_right))
            nc.vector.tensor_copy(hi[:], pos_i)
            then(nc.vector.tensor_scalar(pos.bitcast(I32), cur, 127, None, ALU.bitwise_and))
            nc.vector.tensor_copy(lo[:], pos.bitcast(I32))
            then(nc.vector.tensor_scalar(diag[:], ident[:], small[:, 1:2], None, ALU.mult))
            dve.wait_ge(s_bias, 32)
            nc.vector.tensor_tensor(bias[:], bias[:], bias2[:], ALU.add).then_inc(s_const, 1)
            dve.wait_ge(s_const, 1)

            A_PRE = NT - A_LOOP

            def a_out(done, tile):
                dve.wait_ge(s_amm, done + 1)
                nc.vector.tensor_tensor(tile, ps_a[:, 0, :], bias[:], ALU.add).then_inc(s_aev, 1)

            for t in range(A_LOOP, NT):
                a_out(t - A_LOOP, a_sb[:, t, :])
            dve.wait_ge(s_flags, 1)
            then(nc.vector.tensor_scalar(carry_on[:], ps_b[:, 0, 0:P], -2.0, 1.0, ALU.mult, ALU.add))
            nc.vector.tensor_scalar(carry_on[:], carry_on[:], FLT_MAX, None, ALU.mult).then_inc(s_const, 1)

            def fold_turn(turn, gathered, ahead, first, mixed=None, aside={}):
                if not first:
                    dve.wait_ge(s_fold, turn * U)
                nc.vector.tensor_copy(reset_now[:], reset[:, bass.ds(turn * U, U)]).then_inc(s_reset, 1)
                dve.wait_ge(s_reset, turn + 1)
                for g, n in enumerate(GROUPS):
                    if mixed is None:
                        by_group = 16 * (n - (g == NG - 1))
                        dve.wait_ge(s_got[g], gathered * by_group + by_group)
                    else:
                        dve.wait_ge(s_now, mixed * NG + (g + 1))
                    if g >= 2:
                        dve.wait_ge(s_copied[g - 2], turn + 1)
                    elif not first:
                        dve.wait_ge(s_copied[g + 2], turn)
                    for s in range(n):
                        k = START[g] + s
                        former = acc[:, ACC0[g] + s - 1, :] if s else hist[:, (k - 1) % U, :]
                        new = acc[:, ACC0[g] + s, :] if s < n - 1 else hist[:, k, :]
                        row = rows[:, k, :] if mixed is None else converted_rows[:, CONVERTED0[g % 2] + s, :]
                        if k == U - 1 and mixed is None:
                            dve.wait_ge(s_got_end, gathered * 16 + 16)
                        if s == n - 1 and not first:
                            dve.wait_ge(s_hout[g], turn * 16)
                        if not first or k:
                            dve.wait_ge(s_fold, turn * U + k)
                        nc.vector.scalar_tensor_tensor(new, former, reset_now[:, k:k + 1], row,
                                                       ALU.min, ALU.max).then_inc(s_fold, 1)
                    if mixed is None:
                        dve.wait_ge(s_fold, turn * U + (START[g] + n))
                        nc.vector.tensor_copy(stage[:, START[g]:START[g] + n],
                                              idx[:, bass.ds((turn + ahead) * U + START[g], n)]
                                              ).then_inc(s_stage[g], 1)
                    if g in aside:
                        aside[g]()

            def one_hots(share, first):
                if not first:
                    dve.wait_ge(s_hotused, share)
                nc.vector.tensor_tensor(hot_hi[:], cols_b[:, 0:NT].unsqueeze(1).broadcast_to([P, U, NT]),
                                        hi[:, bass.ds(share * U, U)].unsqueeze(2).broadcast_to([P, U, NT]),
                                        ALU.is_equal)
                nc.vector.tensor_tensor(hot_lo[:], cols_b[:].unsqueeze(1).broadcast_to([P, U, P]),
                                        lo[:, bass.ds(share * U, U)].unsqueeze(2).broadcast_to([P, U, P]),
                                        ALU.is_equal).then_inc(s_hot, 1)

            def a_at(t):
                return a_sb[:, bass.ds(t, 1), :].rearrange("p a d -> p (a d)")

            def beside(i, first):
                def tile(j):
                    a_out(i * A_BESIDE + (A_PRE + j), a_at(i * A_BESIDE + j))

                assert A_BESIDE == 2
                fold_turn(i, i, 1, first, aside={0: lambda: tile(0), 1: lambda: one_hots(i, first),
                                                 3: lambda: tile(1)})

            beside(0, True)
            with dve.Fori(1, BESIDE) as i:
                beside(i, False)
            with dve.Fori(0, MIX) as i:
                def tile_and_share(j):
                    a_out(i * A_MIX + (A_PRE + A_BESIDE * BESIDE + j), a_at(i * A_MIX + (A_BESIDE * BESIDE + j)))
                    one_hots(i * MIX_SHARES + (BESIDE + j), False)

                assert A_MIX == MIX_SHARES == MIX_TURNS - 2 and MIX_TURNS == 5
                fold_turn(i * 5 + MIX_AT, i * 4 + BESIDE, 2, False)
                fold_turn(i * 5 + (MIX_AT + 1), None, None, False, mixed=i)
                for q in range(3):
                    fold_turn(i * 5 + (MIX_AT + 2 + q), i * 4 + (BESIDE + 1 + q), 1, False,
                              aside={2: lambda: tile_and_share(q)})
            nc.vector.memset(x_sb[96:P, NT - 1, :], 0.0).then_inc(s_pad, 1)
            with dve.Fori(0, COUNT) as i:
                def share(r):
                    one_hots(i * 2 + (BESIDE + MIX_SHARES * MIX + r), False)

                fold_turn(i + COUNT_AT, i + (BESIDE + (MIX_TURNS - 1) * MIX), 1, False,
                          aside={1: lambda: share(0), 3: lambda: share(1)})

            def sum_counts():
                dve.wait_ge(s_hotused, TURNS + 1)
                nc.vector.tensor_copy(counts[0:NT, :], ps_h[0:NT, 0, 0:P]).then_inc(s_ends, 1)
                nc.vector.tensor_tensor_scan(csum[0:NT, :], ones[0:NT, :], ps_h[0:NT, 0, 0:P], 0.0, ALU.mult,
                                             ALU.add).then_inc(s_csum, 1)

            def find_ends():
                dve.wait_ge(s_csum, 1)
                dve.wait_ge(s_before, 1)
                then(nc.vector.tensor_scalar(small[0:NT, 7:8], ps_a[0:NT, 0, 0:1], -1.0, None, ALU.add))
                nc.vector.tensor_scalar(ends[0:NT, :], csum[0:NT, :], small[0:NT, 7:8], 0.0, ALU.add,
                                        ALU.max).then_inc(s_ends, 1)

            def by_node():
                dve.wait_ge(s_turned, 2)
                nc.vector.tensor_copy(end_row[:], ps_a[:, 0, 0:NT])
                then(nc.vector.tensor_scalar(has[:], ps_h[:, 0, 0:NT], 0.5, 2.0, ALU.is_gt, ALU.mult))
                then(nc.vector.tensor_scalar(has[:], has[:], 1.0, FLT_MAX, ALU.subtract, ALU.mult))

            fold_turn(LAST_AT, GATHERED - LAST, 1, False, aside={1: sum_counts, 2: find_ends, 3: by_node})

            def mask(t):
                nc.vector.tensor_scalar(a_at(t), a_at(t), has[:, bass.ds(t, 1)], None, ALU.min)

            MASKED = NT // (LAST - 1)
            with dve.Fori(0, LAST - 1) as i:
                def masks(these):
                    for j in these:
                        mask(i * MASKED + j)

                fold_turn(i + (LAST_AT + 1), i + (GATHERED - LAST + 1), 1, False,
                          aside={0: lambda: masks(range(0, 2 * MASKED // 3)),
                                 1: lambda: masks(range(2 * MASKED // 3, MASKED))})
            for t in range(MASKED * (LAST - 1), NT):
                nc.vector.tensor_scalar(a_sb[:, t, :], a_sb[:, t, :], has[:, t:t + 1], None, ALU.min)
            nc.vector.memset(small[:, 8:9], 0.0).then_inc(s_masked, 1)

            dve.wait_ge(s_lastt, 1)
            for k in range(KC):
                nc.vector.tensor_tensor_scan(scanned[:, k, 1:P + 1], carry_on[:], ps_t[:, 0, k * P:(k + 1) * P],
                                             -FLT_MAX, ALU.min, ALU.max).then_inc(s_scan, 1)
            dve.wait_ge(s_carry, 1)
            dve.wait_ge(s_fixin, 16)
            nc.vector.tensor_tensor(fix[:], fix[:], ps_b[:, 0, :], ALU.max).then_inc(s_fixed, 1)


            def finish(before, o, first, tiles, between=None):
                these = slice(first, first + tiles)
                dve.wait_ge(s_sd, before + 1)
                nc.vector.reciprocal(rstd[:, these], sd[:, these]).then_inc(s_o, 1)
                if between is not None:
                    between()
                dve.wait_ge(s_o, o + 1)
                nc.vector.scalar_tensor_tensor(shift[:, these], meanvar[:, these, 0], -1.0, rstd[:, these],
                                               ALU.mult, ALU.mult).then_inc(s_scale, 1)

            def tiles_out(o, y, xs, first, tiles, arrived, count, former=None, written=None):
                z = hist[:, first:first + tiles, :]
                dve.wait_ge(arrived, count)
                nc.vector.scalar_tensor_tensor(y, y, FLT_MAX, y, ALU.is_le, ALU.mult).then_inc(s_o, 1)

                def add_x():
                    if written is not None:
                        dve.wait_ge(*written)
                    dve.wait_ge(s_o, o + 1)
                    nc.vector.scalar_tensor_tensor(z, y, 0.0, xs, ALU.max, ALU.add).then_inc(s_o, 1)

                if former is None:
                    add_x()
                    o = o + 2
                else:
                    before, slot, n = former
                    finish(before, o + 1, slot, n, between=add_x)
                    o = o + 3
                dve.wait_ge(s_o, o)
                for j in range(tiles):
                    nc.vector.bn_stats(stats[:, first + j, :], z[:, j, :]).then_inc(s_o, 1)
                dve.wait_ge(s_o, o + tiles)
                dve.nop(nofuse=True)
                for j in range(tiles):
                    last = nc.vector.bn_aggr(meanvar[:, first + j, :], stats[:, first + j, :])
                    last.then_inc(s_o if j < tiles - 1 else s_var, 1)

            SHORT = 3
            PER_QUARTER = 2 + 2 * QUARTER
            dve.wait_ge(s_x, 16 * (X_LOADS + 1))
            for g in range(NG):
                dve.wait_ge(s_hout[g], 16 * TURNS)
            tiles_out(0, a_sb[:, NT - 1:NT, :], x_sb[:, NT - 1:NT, :], U - 1, 1, s_end_short, 16)

            def out_turn(c, first):
                for q in range(4):
                    o = c * (4 * PER_QUARTER) + (q * PER_QUARTER + SHORT)
                    these = bass.ds(c * 4 * QUARTER + q * QUARTER, QUARTER)
                    if first and q == 0:
                        former = (0, U - 1, 1)
                    else:
                        former = (c * 4 + q, (q - 1) % 4 * QUARTER, QUARTER)
                    tiles_out(o, a_sb[:, these, :], x_sb[:, these, :], q * QUARTER, QUARTER, s_end[q],
                              (c + 1) * (16 * QUARTER), former, None if first else (s_out[q], c * 16))

            out_turn(0, True)
            with dve.Fori(1, OUT_TURNS) as c:
                out_turn(c, False)
            finish(4 * OUT_TURNS, 4 * OUT_TURNS * PER_QUARTER + SHORT, 3 * QUARTER, QUARTER)


_INS = ["x", "xt", "src", "dst", "theta_t", "phi_t", "theta_b", "phi_b"]


def kernel(x, src, dst, L0_gnn_theta_w, L0_gnn_theta_b, L0_gnn_phi_w, L0_gnn_phi_b):
    import numpy as np
    import concourse.bacc as bacc
    from concourse.bass_utils import run_bass_kernel_spmd

    x = np.asarray(x)
    n, d = x.shape
    tiles = (n + P - 1) // P
    padded = np.zeros((tiles * P, d), x.dtype)
    padded[:n] = x
    xt = padded.reshape(tiles, P, d // P, P).transpose(0, 3, 2, 1)
    arrays = {
        "x": x, "xt": xt, "src": np.asarray(src), "dst": np.asarray(dst),
        "theta_t": np.asarray(L0_gnn_theta_w).T, "phi_t": np.asarray(L0_gnn_phi_w).T,
        "theta_b": np.asarray(L0_gnn_theta_b), "phi_b": np.asarray(L0_gnn_phi_b),
    }
    nc = bacc.Bacc("TRN2", target_bir_lowering=False, num_devices=1)
    ins, args = {}, []
    for name in _INS:
        a = np.ascontiguousarray(arrays[name])
        ins[f"in_{name}"] = a
        args.append(nc.dram_tensor(f"in_{name}", a.shape, mybir.dt.from_np(a.dtype), kind="ExternalInput").ap())
    out = nc.dram_tensor("out", (n, d), F32, kind="ExternalOutput").ap()
    build(nc, *args, out)
    r = run_bass_kernel_spmd(nc, [ins], core_ids=[0])
    return r.results[0]["out"]
```
